# Optimizing a Trainium2 kernel written in Bass

```python
import numpy as np
import jax
import jax.numpy as jnp

def _softmax(x, axis=-1):
    return jax.nn.softmax(x, axis=axis)

def _gelu(x):
    return jax.nn.gelu(x, approximate=True)

def _silu(x):
    return jax.nn.silu(x)

def _sigmoid(x):
    return jax.nn.sigmoid(x)

def _layernorm(x, axis=-1, eps=1e-05):
    m = jnp.mean(x, axis=axis, keepdims=True)
    v = jnp.var(x, axis=axis, keepdims=True)
    return (x - m) / jnp.sqrt(v + eps)

def _scatter_add(tgt, idx, src, axis=0):
    return tgt.at[idx].add(src)

def _segment_sum(src, seg, n):
    return jax.ops.segment_sum(src, seg, n)
kernel_name = 'mk_macaron_d1_jaxref_r2_359466'

def setup_inputs(seed: int=0):
    np.random.seed(seed)
    _w = jnp.asarray

    def _L0_attn_setup():
        import jax, jax.numpy as jnp
        import numpy as np
        DIM = 512
        MULT = 1
        HID = DIM * MULT
        C = 8.0
        key = jax.random.key(seed)
        k_x, k_wa, k_wx, k_lam = jax.random.split(key, 4)
        B, T = (8, 2048)
        x = jax.random.normal(k_x, (B, T, DIM), dtype=jnp.float32)
        std = DIM ** (-0.5)
        Wa = jax.random.normal(k_wa, (HID, DIM), dtype=jnp.float32) * std
        Wx = jax.random.normal(k_wx, (HID, DIM), dtype=jnp.float32) * std
        ba = jnp.zeros((HID,), dtype=jnp.float32)
        bx = jnp.zeros((HID,), dtype=jnp.float32)
        lo = float(np.log(0.9 / 0.1))
        hi = float(np.log(0.999 / 0.001))
        Lam = jax.random.uniform(k_lam, (HID,), dtype=jnp.float32, minval=lo, maxval=hi)
        return {'x': x, 'Wa': Wa, 'Wx': Wx, 'ba': ba, 'bx': bx, 'Lam': Lam}
    _L0_attn_in = _L0_attn_setup()

    def _L0_ffn_setup():
        import jax, jax.numpy as jnp
        import numpy as np
        D_MODEL = 512
        DEPTH = 8
        M = 2 ** DEPTH
        N_INTERNAL = M - 1
        B, T = (8, 2048)

        def _leaf_probs(gate):
            BT = gate.shape[0]
            lp = jnp.ones((BT, M), dtype=gate.dtype)
            for level in range(DEPTH):
                n = 2 ** level
                half = M // (2 * n)
                g = gate[:, n - 1:2 * n - 1]
                f = jnp.stack([1.0 - g, g], axis=-1)
                f = jnp.broadcast_to(f[..., None], (BT, n, 2, half))
                lp = lp * f.reshape(BT, M)
            return lp
        key = jax.random.key(seed)
        ks = jax.random.split(key, 7)
        x = jax.random.normal(ks[0], (B, T, D_MODEL), dtype=jnp.float32)
        Wq = jax.random.normal(ks[1], (D_MODEL, D_MODEL), dtype=jnp.float32) * 0.02
        routers = jax.random.normal(ks[2], (N_INTERNAL, D_MODEL), dtype=jnp.float32) * 0.02
        leaf_keys = jax.random.normal(ks[3], (M, D_MODEL), dtype=jnp.float32) * 0.02
        leaf_values = jax.random.normal(ks[4], (M, D_MODEL), dtype=jnp.float32) * 0.02
        Wout_w = jax.random.normal(ks[5], (D_MODEL, D_MODEL), dtype=jnp.float32) * 0.02
        Wout_b = jax.random.normal(ks[6], (D_MODEL,), dtype=jnp.float32) * 0.02
        return {'x': x, 'Wq': Wq, 'routers': routers, 'leaf_keys': leaf_keys, 'leaf_values': leaf_values, 'Wout_w': Wout_w, 'Wout_b': Wout_b}
    _L0_ffn_in = _L0_ffn_setup()
    _d = {'L0_attn_x': _L0_attn_in['x'], 'L0_attn_Wa': _L0_attn_in['Wa'], 'L0_attn_Wx': _L0_attn_in['Wx'], 'L0_attn_ba': _L0_attn_in['ba'], 'L0_attn_bx': _L0_attn_in['bx'], 'L0_attn_Lam': _L0_attn_in['Lam'], 'L0_ffn_Wq': _L0_ffn_in['Wq'], 'L0_ffn_routers': _L0_ffn_in['routers'], 'L0_ffn_leaf_keys': _L0_ffn_in['leaf_keys'], 'L0_ffn_leaf_values': _L0_ffn_in['leaf_values'], 'L0_ffn_Wout_w': _L0_ffn_in['Wout_w'], 'L0_ffn_Wout_b': _L0_ffn_in['Wout_b']}
    _x0 = _d['L0_attn_x']
    _d['L0_attn_x'] = jax.random.normal(jax.random.fold_in(jax.random.key(seed), 1), (8, 2048, 512), dtype=_x0.dtype)
    del _x0
    return _d

def reference(L0_attn_x, L0_attn_Wa, L0_attn_Wx, L0_attn_ba, L0_attn_bx, L0_attn_Lam, L0_ffn_Wq, L0_ffn_routers, L0_ffn_leaf_keys, L0_ffn_leaf_values, L0_ffn_Wout_w, L0_ffn_Wout_b):

    def _L0_attn_ref(x, Wa, Wx, ba, bx, Lam):
        import jax, jax.numpy as jnp
        import numpy as np
        DIM = 512
        MULT = 1
        HID = DIM * MULT
        C = 8.0
        r = jax.nn.sigmoid(jnp.einsum('btd,dh->bth', x, Wa) + ba)
        i = jax.nn.sigmoid(jnp.einsum('btd,dh->bth', x, Wx) + bx)
        a = jax.nn.sigmoid(Lam)
        at = a * jnp.exp(-r * jnp.log(jnp.asarray(C, x.dtype)))
        bt = jnp.sqrt(1.0 - at * at) * (i * x)

        def combine(e1, e2):
            a1, b1 = e1
            a2, b2 = e2
            return (a2 * a1, a2 * b1 + b2)
        _, y = jax.lax.associative_scan(combine, (at, bt), axis=1)
        return y

    def _L0_ffn_ref(x, Wq, routers, leaf_keys, leaf_values, Wout_w, Wout_b):
        import jax, jax.numpy as jnp
        import numpy as np
        D_MODEL = 512
        DEPTH = 8
        M = 2 ** DEPTH
        N_INTERNAL = M - 1
        B, T = (8, 2048)

        def _leaf_probs(gate):
            BT = gate.shape[0]
            lp = jnp.ones((BT, M), dtype=gate.dtype)
            for level in range(DEPTH):
                n = 2 ** level
                half = M // (2 * n)
                g = gate[:, n - 1:2 * n - 1]
                f = jnp.stack([1.0 - g, g], axis=-1)
                f = jnp.broadcast_to(f[..., None], (BT, n, 2, half))
                lp = lp * f.reshape(BT, M)
            return lp
        Bv, Tv, d = x.shape
        q = jnp.einsum('btd,ed->bte', x, Wq)
        q_flat = q.reshape(Bv * Tv, d)
        gate = jax.nn.sigmoid(q_flat @ routers.T)
        leaf_prob = _leaf_probs(gate)
        ret = (leaf_prob @ leaf_values).reshape(Bv, Tv, d)
        return jnp.einsum('btd,ed->bte', ret, Wout_w) + Wout_b
    x = L0_attn_x
    x = x + 0.5 * _L0_ffn_ref(_layernorm(x, axis=-1), L0_ffn_Wq, L0_ffn_routers, L0_ffn_leaf_keys, L0_ffn_leaf_values, L0_ffn_Wout_w, L0_ffn_Wout_b)
    x = x + _L0_attn_ref(_layernorm(x, axis=-1), L0_attn_Wa, L0_attn_Wx, L0_attn_ba, L0_attn_bx, L0_attn_Lam)
    x = x + 0.5 * _L0_ffn_ref(_layernorm(x, axis=-1), L0_ffn_Wq, L0_ffn_routers, L0_ffn_leaf_keys, L0_ffn_leaf_values, L0_ffn_Wout_w, L0_ffn_Wout_b)
    return x

_drawn_inputs = setup_inputs


def setup_inputs(seed=0):
    import zlib

    import numpy as np

    out = dict(_drawn_inputs(seed))
    spreads = {'L0_attn_ba': (0.0, 0.8), 'L0_attn_bx': (0.0, 0.577)}
    factors = {'L0_attn_Lam': 8.0,
     'L0_ffn_Wq': 8.0,
     'L0_ffn_routers': 8.0,
     'L0_ffn_leaf_values': 8.0,
     'L0_ffn_Wout_w': 8.0,
     'L0_ffn_Wout_b': 2.965}
    for name, (base, spread) in spreads.items():
        noise = np.random.default_rng([zlib.crc32(name.encode()), seed]).standard_normal(out[name].shape)
        drawn = base * np.exp(spread * noise) if base else spread * noise
        out[name] = jnp.asarray(drawn.astype(out[name].dtype))
    for name, factor in factors.items():
        out[name] = (out[name] * factor).astype(out[name].dtype)
    return out
```

```python
import numpy as np
import concourse.bass as bass
from concourse import mybir
from contextlib import ExitStack


def macaron_kernel(
    nc: bass.Bass,
    x_in: bass.AP,
    w_a: bass.AP,
    w_x: bass.AP,
    b_a: bass.AP,
    b_x: bass.AP,
    lam: bass.AP,
    w_q: bass.AP,
    routers: bass.AP,
    leaf_values: bass.AP,
    w_out: bass.AP,
    b_out: bass.AP,
    out: bass.AP,
):
    fp32, fp16, i32 = mybir.dt.float32, mybir.dt.float16, mybir.dt.int32
    ALU = mybir.AluOpType
    ACT = mybir.ActivationFunctionType
    AX = mybir.AxisListType
    RMAX = bass.bass_isa.ReduceOp.max

    P = 128
    B, T, D = x_in.shape
    NODES = routers.shape[0]
    LEAVES = leaf_values.shape[0]
    HALF = LEAVES // 2
    DEPTH = LEAVES.bit_length() - 1
    KD = D // P
    KL = LEAVES // P
    GT = 512
    TILES = GT // P
    GROUPS = B * T // GT
    PER_SEQ = T // GT
    BANKS = 8
    UNROLL = 4
    FIRST, LOOPS = 4, (GROUPS - 4) // UNROLL - 1
    LAST = FIRST + UNROLL * LOOPS
    assert D == GT and NODES == LEAVES - 1 and KL == 2 and UNROLL % PER_SEQ == 0

    EPS = 1e-5
    LOG_C = float(np.log(8.0))
    XN = 2.0 ** 8
    ROOT = 2.0 ** 7
    HIDDEN_SCALE = ROOT * 2.0 ** (DEPTH - 1)
    TOP = 14
    EXPONENT = 0x7F800000
    ROOT_SCALE = (0.5 / XN) ** 2

    N1_T, Y_T, LOGITS1, N3_T, LEAF1_T, LOGITS3, Y1, LEAF3_T, N2_T = 0, 6, 10, 14, 20, 22, 24, 29, 34
    R_JOB, I_JOB, Y3_JOB = [4, 12, 18, 28], [5, 13, 19, 31], [32, 33, 38, 39]
    JOBS = 40
    Y1_BANK = [(Y1 + t) % BANKS for t in range(TILES)]
    R_BANK, I_BANK, Y3_BANK = ([j % BANKS for j in jobs] for jobs in (R_JOB, I_JOB, Y3_JOB))
    assert JOBS % BANKS == 0

    LOADS = 12
    DVE_SIGN = 1 + (DEPTH - 1)
    DVE_LEAVES = DVE_SIGN + 1
    DVE_SIGN_READ = DVE_LEAVES + 5
    DVE_T1 = DVE_SIGN_READ + 1 + 2 * KD
    DVE_T2 = DVE_T1 + KD
    DVE_PEAK = DVE_T2 + KD + 3 + 8

    x_g = x_in.rearrange("b t d -> (b t) d").rearrange("(g t p) d -> g p t d", t=TILES, p=P)
    out_g = out.rearrange("b t d -> (b t) d").rearrange("(g t p) d -> g p t d", t=TILES, p=P)

    ctx = ExitStack()
    with ctx:
        def sb(name, shape, dt=fp32):
            return ctx.enter_context(nc.sbuf_tensor(name, shape, dt))

        def sem(name):
            return ctx.enter_context(nc.semaphore(name))

        bank = [ctx.enter_context(nc.psum_tensor(f"bank{i}", [P, 512], fp32)) for i in range(BANKS)]

        x_rows = [sb(f"x_rows{i}", [P, TILES, D]) for i in range(2)]
        res = [sb(f"res{i}", [P, TILES, D]) for i in range(UNROLL)]
        norm1 = sb("norm1", [P, TILES, D])
        norm2 = sb("norm2", [P, TILES, D])
        norm3 = sb("norm3", [P, TILES, D])
        n1h, n1l = sb("n1h", [P, KD, GT], fp16), sb("n1l", [P, KD, GT], fp16)
        n3h, n3l = sb("n3h", [P, KD, GT], fp16), sb("n3l", [P, KD, GT], fp16)
        n2h = [sb(f"n2h{i}", [P, KD, GT], fp16) for i in range(2)]
        n2l = [sb(f"n2l{i}", [P, KD, GT], fp16) for i in range(2)]
        n2f = sb("n2f", [P, KD, GT])
        gate1, gate3 = sb("gate1", [P, TILES, LEAVES]), sb("gate3", [P, TILES, LEAVES])
        prob1, prob3 = sb("prob1", [P, TILES, HALF]), sb("prob3", [P, TILES, HALF])
        leaf1, leaf3 = sb("leaf1", [P, TILES, LEAVES]), sb("leaf3", [P, TILES, LEAVES])
        leaf1h, leaf1l = sb("leaf1h", [P, KL, GT], fp16), sb("leaf1l", [P, KL, GT], fp16)
        leaf3h, leaf3l = sb("leaf3h", [P, KL, GT], fp16), sb("leaf3l", [P, KL, GT], fp16)
        tanh_r = [sb(f"tanh_r{i}", [P, GT]) for i in range(2)]
        tanh_i = [sb(f"tanh_i{i}", [P, GT]) for i in range(2)]
        decay = sb("decay", [P, KD, GT])
        root = sb("root", [P, KD, GT])
        state = sb("state", [P, KD, GT])
        carry = sb("carry", [P, KD])

        wah, wal = sb("wah", [P, KD, D], fp16), sb("wal", [P, KD, D], fp16)
        wxh, wxl = sb("wxh", [P, KD, D], fp16), sb("wxl", [P, KD, D], fp16)
        w1h, w1l = sb("w1h", [P, KD, LEAVES], fp16), sb("w1l", [P, KD, LEAVES], fp16)
        w2h, w2l = sb("w2h", [P, KL, D], fp16), sb("w2l", [P, KL, D], fp16)

        ident = sb("ident", [P, P])
        minus_half = sb("minus_half", [P, TILES])
        stats = [sb(f"stats{n}", [P, TILES, nc.vector.BN_STATS_DIM]) for n in (1, 2, 3)]
        moments = [sb(f"moments{n}", [P, TILES, nc.vector.BN_AGGR_DIM]) for n in (1, 2, 3)]
        var_eps = [sb(f"var_eps{n}", [P, TILES]) for n in (1, 2, 3)]
        rstd = [sb(f"rstd{n}", [P, TILES]) for n in (1, 2, 3)]
        neg_mean = [sb(f"neg_mean{n}", [P, TILES]) for n in (1, 2, 3)]
        ba_half, bx_half = sb("ba_half", [P, KD]), sb("bx_half", [P, KD])
        lam_col, log_a = sb("lam_col", [P, KD]), sb("log_a", [P, KD])
        lam_abs, lam_exp, lam_ln = sb("lam_abs", [P, KD]), sb("lam_exp", [P, KD]), sb("lam_ln", [P, KD])
        sign_row, one = sb("sign_row", [1, P]), sb("one", [1, 1])
        sign = sb("sign", [P, 1])
        peak, peak_all, w_scale, w_inv, act_scale = (sb(n, [P, 4]) for n in (
            "peak", "peak_all", "w_scale", "w_inv", "act_scale"))
        W_A, W_X, W_1, W_2 = range(4)
        ffn_scale, root_bias = sb("ffn_scale", [P, 1]), sb("root_bias", [P, 1])

        wq_s, wout_s, wout_t = res[0], res[1], res[2]
        routers_t = res[3][:, 0:2, :].rearrange("p a n -> p (a n)").rearrange("p (k n) -> p k n", k=KD)
        leaves_t = res[3][:, 2:4, :].rearrange("p a n -> p (a n)").rearrange("p (k n) -> p k n", k=KD)
        routers_s = root[:, 0:2, :]
        even_s, odd_s = root[:, 2, :], root[:, 3, :]
        wa_s, wx_s = decay, state
        w1_s = norm3[:, 0:2, :].rearrange("p a n -> p (a n)").rearrange("p (k n) -> p k n", k=KD)
        w2_s = norm3[:, 2:4, :]
        bias_s = norm2[:, 0, :]
        abs_s = n2f

        loaded_w = sem("loaded_w")
        loaded_x = [sem("loaded_x0"), sem("loaded_x1")]
        stored = [sem(f"stored{i}") for i in range(UNROLL)]
        setup_pool, setup_pe, setup_act, weights_ready = map(sem, (
            "setup_pool", "setup_pe", "setup_act", "weights_ready"))
        setup_dve, passed = sem("setup_dve"), sem("waits_passed")
        n1_t, n2_t, n3_t = map(sem, ("n1_transposed", "n2_transposed", "n3_transposed"))
        logits1, logits3 = map(sem, ("logits1", "logits3"))
        leaf1_t, leaf3_t = map(sem, ("leaf1_transposed", "leaf3_transposed"))
        ffn1, ffn3 = map(sem, ("ffn1_out", "ffn3_out"))
        r_out, i_out, y_t = map(sem, ("r_preact", "i_preact", "y_transposed"))
        n1_hi, n2_hi, n3_hi = map(sem, ("n1_hi", "n2_hi", "n3_hi"))
        tanh1, tanh3 = map(sem, ("gates1", "gates3"))
        leaf1_hi, leaf3_hi = map(sem, ("leaf1_hi", "leaf3_hi"))
        r_tanh, i_tanh, decayed, squared, rest = map(sem, (
            "r_tanh", "i_tanh", "decayed", "squared", "one_minus_square"))
        rooted = sem("rooted")
        n1_lo, n2_lo, n3_lo = map(sem, ("n1_lo", "n2_lo", "n3_lo"))
        leaf1_lo, leaf3_lo = map(sem, ("leaf1_lo", "leaf3_lo"))
        added1, added2, added3 = map(sem, ("added1", "added2", "added3"))
        stat = [sem(f"stat{n}") for n in (1, 2, 3)]
        moment = [sem(f"moment{n}") for n in (1, 2, 3)]
        tree1, tree3 = sem("tree1"), sem("tree3")
        gated, scaled, scanned = map(sem, ("gated", "scaled", "scanned"))
        carried = sem("carried")
        row_scale = [sem(f"row_scale{n}") for n in (1, 2, 3)]
        normed = [sem(f"normed{n}") for n in (1, 2, 3)]
        TREE = 2 * (DEPTH - 1) + 1

        RELEASES = [None] * JOBS
        for lag, jobs, release in (
                (0, range(N1_T, N1_T + KD), n1_lo), (1, R_JOB, r_tanh), (1, I_JOB, i_tanh),
                (2, range(Y_T, Y_T + TILES), added2), (0, range(LOGITS1, LOGITS1 + 2), tanh1),
                (2, range(N3_T, N3_T + KD), n3_lo), (0, range(LEAF1_T, LEAF1_T + KL), leaf1_lo),
                (2, range(LOGITS3, LOGITS3 + 2), tanh3), (0, range(Y1, Y1 + TILES), added1),
                (2, range(LEAF3_T, LEAF3_T + KL), leaf3_lo), (2, Y3_JOB, added3),
                (0, range(N2_T, N2_T + KD), n2_lo)):
            for k, job in enumerate(jobs):
                assert RELEASES[job] is None
                RELEASES[job] = (lag, release, len(jobs), k)

        block = ctx.enter_context(nc.Block())

        def wait(eng, semaphore, per_group, g, k):
            if isinstance(g, int) and (g < 0 or per_group * g + k <= 0):
                return
            eng.wait_ge(semaphore, per_group * g + k)

        def pass_waits(eng):
            eng.sem_inc(passed, 1)

        def steps(eng, emit):
            def at(s):
                emit(s, s % UNROLL, s < GROUPS, 1 <= s <= GROUPS, 2 <= s, s + 1 < GROUPS)
            for s in range(FIRST):
                at(s)
            with eng.Fori(0, LOOPS) as i:
                for k in range(UNROLL):
                    emit(UNROLL * i + (FIRST + k), (FIRST + k) % UNROLL, True, True, True, True)
            for s in range(LAST, GROUPS + 2):
                at(s)

        @block.sync
        def _(sp):
            sp.dma_start(x_rows[0][:, :, :], x_g[0, :, :, :]).then_inc(loaded_x[0], 16)
            sp.dma_start(x_rows[1][:, :, :], x_g[1, :, :, :]).then_inc(loaded_x[1], 16)

            def load(g, parity):
                wait(sp, added1, TILES, g - 2, TILES)
                sp.dma_start(x_rows[parity][:, :, :], x_g[g, :, :, :]).then_inc(loaded_x[parity], 16)

            def store(g, slot):
                for h in range(2):
                    wait(sp, added3, TILES, g, 2 * h + 2)
                    sp.dma_start(out_g[g, :, 2 * h:2 * h + 2, :], res[slot][:, 2 * h:2 * h + 2, :])\
                      .then_inc(stored[slot], 16)

            def step(s, m, a, b, c, n):
                if not isinstance(s, int) or s + 2 < GROUPS:
                    load(s + 2, m % 2)
                if c:
                    store(s - 2, (m - 2) % UNROLL)

            steps(sp, step)
            for slot in range(UNROLL):
                sp.wait_ge(stored[slot], 32 * (GROUPS // UNROLL))

        @block.gpsimd
        def _(pool):
            nc.gpsimd.memset(ident[:, :], 0.0).then_inc(setup_pool, 1)
            nc.gpsimd.memset(minus_half[:, :], -0.5).then_inc(setup_pool, 1)
            pool.wait_ge(setup_pool, 2)
            nc.gpsimd.affine_select(out=ident[:, :], in_=ident[:, :], compare_op=ALU.not_equal, fill=1.0,
                                    base=0, pattern=[[-1, P]], channel_multiplier=1).then_inc(setup_pool, 1)
            pool.wait_ge(setup_dve, DVE_PEAK)
            nc.gpsimd.partition_all_reduce(peak_all[:, :], peak[:, :], P, RMAX).then_inc(setup_pool, 1)

            def normalise(n, rows, g, into, free):
                mv = moments[n]
                wait(pool, moment[n], TILES, g, TILES)
                wait(pool, normed[n], TILES, g, 0)
                pass_waits(pool)
                nc.gpsimd.tensor_scalar(var_eps[n][:, :], mv[:, :, 1], XN ** -2, EPS * XN ** -2,
                                        ALU.mult, ALU.add).then_inc(row_scale[n], 1)
                nc.gpsimd.tensor_scalar(neg_mean[n][:, :], mv[:, :, 0], -1.0, 0.0,
                                        ALU.mult, ALU.add).then_inc(row_scale[n], 1)
                wait(pool, row_scale[n], 3, g, 2)
                nc.gpsimd.tensor_tensor(rstd[n][:, :], var_eps[n][:, :], minus_half[:, :],
                                        ALU.pow).then_inc(row_scale[n], 1)
                wait(pool, row_scale[n], 3, g, 3)
                wait(pool, free, KD, g, 0)
                pass_waits(pool)
                for t in range(TILES):
                    nc.gpsimd.tensor_scalar(into[:, t, :], rows[:, t, :], neg_mean[n][:, t:t + 1],
                                            rstd[n][:, t:t + 1], ALU.add, ALU.mult).then_inc(normed[n], 1)

            pool.wait_ge(weights_ready, 1)
            normalise(0, x_rows[0], 0, norm1, n1_t)

            def step(s, m, a, b, c, n):
                if c:
                    normalise(2, res[(m - 2) % UNROLL], s - 2, norm3, n3_t)
                if n:
                    normalise(0, x_rows[(m + 1) % 2], s + 1, norm1, n1_t)
                if a:
                    normalise(1, res[m], s, norm2, n2_t)

            steps(pool, step)

        @block.scalar
        def _(act):
            act.dma_start(wa_s[:, :, :], w_a.rearrange("(k p) h -> p k h", p=P)).then_inc(loaded_w, 16)
            act.dma_start(wx_s[:, :, :], w_x.rearrange("(k p) h -> p k h", p=P)).then_inc(loaded_w, 16)
            act.dma_start(routers_s[:, 0, :], routers[0:P, :]).then_inc(loaded_w, 16)
            act.dma_start(routers_s[0:NODES - P, 1, :], routers[P:NODES, :]).then_inc(loaded_w, 16)
            halves = leaf_values.rearrange("(k two) d -> two k d", two=2)
            act.dma_start(even_s, halves[0, :, :]).then_inc(loaded_w, 16)
            act.dma_start(odd_s, halves[1, :, :]).then_inc(loaded_w, 16)
            act.dma_start(wq_s[:, :, :], w_q.rearrange("(k p) d -> p k d", p=P)).then_inc(loaded_w, 16)
            act.dma_start(wout_s[:, :, :], w_out.rearrange("(k p) d -> p k d", p=P)).then_inc(loaded_w, 16)
            act.dma_start(bias_s, b_out.rearrange("(a d) -> a d", a=1).to_broadcast([P, D]))\
               .then_inc(loaded_w, 16)
            with nc.allow_non_contiguous_dma(reason="512 biases by channel, once"):
                for col, vec in ((ba_half, b_a), (bx_half, b_x), (lam_col, lam)):
                    act.dma_start(col[:, :], vec.rearrange("(c p) -> p c", p=P)).then_inc(loaded_w, 16)
            act.wait_ge(loaded_w, 16 * LOADS)
            nc.scalar.activation(lam_abs[:, :], lam_col[:, :], ACT.Abs).then_inc(setup_act, 1)
            act.wait_ge(setup_act, 1)
            nc.scalar.activation(lam_exp[:, :], lam_abs[:, :], ACT.Exp, scale=-1.0).then_inc(setup_act, 1)
            act.wait_ge(setup_act, 2)
            nc.scalar.activation(lam_ln[:, :], lam_exp[:, :], ACT.Ln, bias=1.0).then_inc(setup_act, 1)
            act.wait_ge(weights_ready, 1)

            def split_hi(src_sem, per, base, g, k, hi, hi_sem):
                wait(act, src_sem, per, g, k + 1)
                nc.scalar.activation(hi, bank[(base + k) % BANKS][:, :], ACT.Copy).then_inc(hi_sem, 1)

            def r_gate(g, c):
                wait(act, r_out, KD, g, c + 1)
                wait(act, decayed, KD, g, c - 1)
                nc.scalar.activation(tanh_r[c % 2][:, :], bank[R_BANK[c]][:, :], ACT.Tanh,
                                     bias=ba_half[:, c:c + 1],
                                     scale=act_scale[:, W_A:W_A + 1]).then_inc(r_tanh, 1)

            def r_decay(g, c):
                wait(act, r_tanh, KD, g, c + 1)
                wait(act, scanned, KD, g - 1, c + 1)
                nc.scalar.activation(decay[:, c, :], tanh_r[c % 2][:, :], ACT.Exp,
                                     bias=log_a[:, c:c + 1], scale=-0.5 * LOG_C).then_inc(decayed, 1)

            def r_root(g, c):
                wait(act, decayed, KD, g, c + 1)
                wait(act, scaled, KD, g - 1, c + 1)
                nc.scalar.activation(root[:, c, :], decay[:, c, :], ACT.Square).then_inc(squared, 1)
                wait(act, squared, KD, g, c + 1)
                nc.scalar.activation(root[:, c, :], root[:, c, :], ACT.Relu, scale=-ROOT_SCALE,
                                     bias=root_bias[:, :]).then_inc(rest, 1)

            def i_gate(g, c):
                wait(act, i_out, KD, g, c + 1)
                wait(act, gated, KD, g, c - 1)
                nc.scalar.activation(tanh_i[c % 2][:, :], bank[I_BANK[c]][:, :], ACT.Tanh,
                                     bias=bx_half[:, c:c + 1],
                                     scale=act_scale[:, W_X:W_X + 1]).then_inc(i_tanh, 1)

            def tree_gates(g, j, logits, base, gates, tanhs, tree):
                wait(act, logits, 2, g, j + 1)
                wait(act, tree, TREE, g, 0)
                nc.scalar.activation(gates[:, 2 * j:2 * j + 2, :].rearrange("p t n -> p (t n)"),
                                     bank[(base + j) % BANKS][:, :], ACT.Tanh,
                                     scale=act_scale[:, W_1:W_1 + 1]).then_inc(tanhs, 1)

            def step(s, m, a, b, c, n):
                ga, gb, gc = s, s - 1, s - 2
                if a:
                    wait(act, logits1, 2, ga, 0)
                    for k in range(KD):
                        split_hi(n1_t, KD, N1_T, ga, k, n1h[:, k, :], n1_hi)
                if b:
                    r_gate(gb, 0)
                    i_gate(gb, 0)
                    r_decay(gb, 0)
                    r_root(gb, 0)
                if a:
                    for j in range(2):
                        tree_gates(ga, j, logits1, LOGITS1, gate1, tanh1, tree1)
                if b:
                    r_gate(gb, 1)
                    i_gate(gb, 1)
                    r_decay(gb, 1)
                    r_root(gb, 1)
                if c:
                    wait(act, logits3, 2, gc, 0)
                    for k in range(KD):
                        split_hi(n3_t, KD, N3_T, gc, k, n3h[:, k, :], n3_hi)
                if b:
                    r_gate(gb, 2)
                    i_gate(gb, 2)
                    r_decay(gb, 2)
                    r_root(gb, 2)
                if a:
                    wait(act, ffn1, TILES, ga, 0)
                    for k in range(KL):
                        split_hi(leaf1_t, KL, LEAF1_T, ga, k, leaf1h[:, k, :], leaf1_hi)
                if c:
                    for j in range(2):
                        tree_gates(gc, j, logits3, LOGITS3, gate3, tanh3, tree3)
                if b:
                    r_gate(gb, 3)
                    r_decay(gb, 3)
                    r_root(gb, 3)
                if c:
                    wait(act, ffn3, TILES, gc, 0)
                    for k in range(KL):
                        split_hi(leaf3_t, KL, LEAF3_T, gc, k, leaf3h[:, k, :], leaf3_hi)
                if b:
                    i_gate(gb, 3)
                    wait(act, rest, KD, gb, KD)
                    nc.scalar.activation(root[:, :, :], root[:, :, :], ACT.Sqrt).then_inc(rooted, 1)
                if a:
                    wait(act, gated, KD, gb, KD)
                    wait(act, i_out, KD, ga - 2, KD)
                    for k in range(KD):
                        wait(act, n2_t, KD, ga, k + 1)
                        nc.scalar.activation(n2f[:, k, :], bank[(N2_T + k) % BANKS][:, :], ACT.Copy)
                        nc.scalar.activation(n2h[m % 2][:, k, :], bank[(N2_T + k) % BANKS][:, :],
                                             ACT.Copy).then_inc(n2_hi, 1)

            steps(act, step)

        @block.vector
        def _(dve):
            done = [0]

            def link(ins):
                done[0] += 1
                ins.then_inc(setup_dve, 1)
                dve.wait_ge(setup_dve, done[0])

            nc.vector.memset(one[:, :], 1.0)
            nc.vector.memset(root_bias[:, :], ROOT_SCALE)
            link(nc.vector.memset(sign_row[:, :], 1.0))
            for bit in range(DEPTH - 1):
                left = sign_row[0:1, :].rearrange("o (h two l) -> o h two l", two=2, l=2 ** bit)[:, :, 0, :]
                link(nc.vector.tensor_scalar(left, left, -1.0, None, ALU.mult))
            assert done[0] == DVE_SIGN
            dve.wait_ge(loaded_w, 16 * LOADS)
            link(nc.vector.tensor_tensor(odd_s, odd_s, even_s, ALU.subtract))
            assert done[0] == DVE_LEAVES
            link(nc.vector.tensor_scalar(ba_half[:, :], ba_half[:, :], 0.5, None, ALU.mult))
            link(nc.vector.tensor_scalar(bx_half[:, :], bx_half[:, :], 0.5, None, ALU.mult))
            dve.wait_ge(setup_act, 3)
            link(nc.vector.scalar_tensor_tensor(log_a[:, :], lam_col[:, :], 0.0, lam_ln[:, :],
                                                ALU.min, ALU.subtract))
            link(nc.vector.tensor_scalar(log_a[:, :], log_a[:, :], -0.5 * LOG_C, None, ALU.add))
            dve.wait_ge(setup_pe, 1)
            link(nc.vector.tensor_copy(sign[:, :], bank[0][:, 0:1]))
            dve.wait_ge(setup_pe, 2)
            link(nc.vector.memset(routers_t[:, :, NODES:LEAVES], 0.0))
            for k in range(KD):
                link(nc.vector.tensor_copy(routers_t[:, k, 0:NODES], bank[k][:, 0:NODES]))
                link(nc.vector.tensor_copy(leaves_t[:, k, :], bank[KD + k][:, 0:LEAVES]))
            assert done[0] == DVE_T1
            dve.wait_ge(setup_pe, 3)
            for k in range(KD):
                link(nc.vector.tensor_copy(wout_t[:, k, :], bank[k][:, :]))
            assert done[0] == DVE_T2
            dve.wait_ge(setup_pe, 4)
            for k in range(KD):
                link(nc.vector.tensor_copy(w1_s[:, k, :], bank[KD + k][:, 0:LEAVES]))
            dve.wait_ge(setup_pe, 5)
            link(nc.vector.tensor_tensor(w2_s[:, 0, :], bank[0][:, :], bias_s, ALU.add))
            link(nc.vector.tensor_scalar(w2_s[:, 0, :], w2_s[:, 0, :], sign[:, :], 2.0, ALU.mult, ALU.mult))
            link(nc.vector.tensor_scalar(w2_s[:, 1, :], bank[1][:, :], sign[:, :], None, ALU.mult))
            whole = {W_A: (wa_s[:, :, :], wah[:, :, :], wal[:, :, :]),
                     W_X: (wx_s[:, :, :], wxh[:, :, :], wxl[:, :, :]),
                     W_1: (w1_s, w1h[:, :, :], w1l[:, :, :]),
                     W_2: (w2_s, w2h[:, :, :], w2l[:, :, :])}
            for j, (w, _, _) in whole.items():
                a_, n_ = w.shape[1], w.shape[2]
                size = abs_s[:, :, :].rearrange("p a n -> p (a n)")[:, 0:a_ * n_]
                size = size.rearrange("p (a n) -> p a n", a=a_)
                link(nc.vector.scalar_tensor_tensor(size, w, -1.0, w, ALU.mult, ALU.max))
                link(nc.vector.reduce_max(peak[:, j:j + 1], size, AX.XY))
            assert done[0] == DVE_PEAK
            dve.wait_ge(setup_pool, 4)
            link(nc.vector.tensor_scalar(peak_all[:, :], peak_all[:, :], 2.0 ** -96, 2.0 ** 96,
                                         ALU.max, ALU.min))
            link(nc.vector.tensor_scalar(w_inv[:, :].bitcast(i32), peak_all[:, :].bitcast(i32),
                                         EXPONENT, None, ALU.bitwise_and))
            link(nc.vector.tensor_scalar(w_scale[:, :].bitcast(i32), w_inv[:, :].bitcast(i32),
                                         EXPONENT, None, ALU.bitwise_xor))
            link(nc.vector.tensor_scalar(w_scale[:, :], w_scale[:, :], 2.0 ** (TOP - 1), None, ALU.mult))
            link(nc.vector.tensor_scalar(w_inv[:, :], w_inv[:, :], 2.0 ** -TOP, None, ALU.mult))
            link(nc.vector.tensor_scalar(act_scale[:, :], w_inv[:, :], 0.5 / XN, None, ALU.mult))
            link(nc.vector.tensor_scalar(ffn_scale[:, :], w_inv[:, W_2:W_2 + 1],
                                         0.5 / (2.0 * HIDDEN_SCALE), None, ALU.mult))
            for j, (w, hi, lo) in whole.items():
                link(nc.vector.tensor_scalar(hi, w, w_scale[:, j:j + 1], None, ALU.mult))
                for k in range(w.shape[1]):
                    link(nc.vector.scalar_tensor_tensor(lo[:, k, :], w[:, k, :], w_scale[:, j:j + 1],
                                                        hi[:, k, :], ALU.mult, ALU.subtract))
            nc.vector.memset(carry[:, :], 0.0).then_inc(weights_ready, 1)

            def split_lo(hi_sem, per, base, g, k, hi, lo, lo_sem):
                wait(dve, hi_sem, per, g, k + 1)
                nc.vector.tensor_tensor(lo, bank[(base + k) % BANKS][:, :], hi, ALU.subtract)\
                  .then_inc(lo_sem, 1)

            def row_stats(n, g, t, rows):
                nc.vector.bn_stats(stats[n][:, t, :], rows[:, t, :]).then_inc(stat[n], 1)

            def row_moments(n, g):
                wait(dve, normed[n], TILES, g, 0)
                wait(dve, stat[n], TILES, g, TILES)
                pass_waits(dve)
                for t in range(TILES):
                    nc.vector.bn_aggr(moments[n][:, t, :], stats[n][:, t, :]).then_inc(moment[n], 1)

            def add_and_stats(n, g, base, ffn, added, rows_in, rows, scale):
                for t in range(TILES):
                    wait(dve, ffn, TILES, g, t + 1)
                    src = bank[(base + t) % BANKS][:, :]
                    if scale is None:
                        nc.vector.tensor_tensor(rows[:, t, :], src, rows_in[:, t, :], ALU.add).then_inc(added, 1)
                    else:
                        nc.vector.scalar_tensor_tensor(rows[:, t, :], src, scale, rows_in[:, t, :],
                                                       ALU.mult, ALU.add).then_inc(added, 1)
                    if t:
                        wait(dve, added, TILES, g, t)
                        row_stats(n, g, t - 1, rows)
                wait(dve, added, TILES, g, TILES)
                row_stats(n, g, TILES - 1, rows)
                row_moments(n, g)

            def tree(g, gates, probs, leaf, tanhs, tree_sem, leaf_t):
                wait(dve, tanhs, 2, g, 2)
                count = 0
                for level in range(DEPTH - 1):
                    n = 2 ** level
                    t = gates[:, :, n - 1:2 * n - 1]
                    if level:
                        wait(dve, tree_sem, TREE, g, count)
                    if level == DEPTH - 2:
                        wait(dve, leaf_t, KL, g, 0)
                        under = leaf[:, :, 0:HALF]
                    else:
                        under = probs[:, :, 2 * n:4 * n]
                    under = under.rearrange("p t (n two) -> p t n two", two=2)
                    for side, sign_of in ((1, 1.0), (0, -1.0)):
                        if level == 0:
                            nc.vector.tensor_scalar(under[:, :, :, side], t, sign_of, ROOT, ALU.add, ALU.mult)\
                              .then_inc(tree_sem, 1)
                        else:
                            nc.vector.scalar_tensor_tensor(under[:, :, :, side], t, sign_of,
                                                           probs[:, :, n:2 * n], ALU.add, ALU.mult)\
                              .then_inc(tree_sem, 1)
                        count += 1
                wait(dve, tree_sem, TREE, g, count)
                nc.vector.scalar_tensor_tensor(leaf[:, :, HALF:LEAVES], gates[:, :, HALF - 1:NODES], 1.0,
                                               leaf[:, :, 0:HALF], ALU.add, ALU.mult).then_inc(tree_sem, 1)

            def gate_input(g, c):
                wait(dve, i_tanh, KD, g, c + 1)
                if c == 0:
                    wait(dve, y_t, TILES, g, 0)
                nc.vector.scalar_tensor_tensor(state[:, c, :], tanh_i[c % 2][:, :], 1.0, n2f[:, c, :],
                                               ALU.add, ALU.mult).then_inc(gated, 1)

            def scan(g, first):
                wait(dve, rooted, 1, g, 1)
                for c in range(KD):
                    wait(dve, gated, KD, g, c + 1)
                    nc.vector.tensor_tensor(state[:, c, :], state[:, c, :], root[:, c, :], ALU.mult)\
                      .then_inc(scaled, 1)
                if not first:
                    wait(dve, carried, 1, g, 0)
                for c in range(KD):
                    wait(dve, scaled, KD, g, c + 1)
                    nc.vector.tensor_tensor_scan(state[:, c, :], decay[:, c, :], state[:, c, :],
                                                 0.0 if first else carry[:, c:c + 1],
                                                 ALU.mult, ALU.add).then_inc(scanned, 1)
                wait(dve, scanned, KD, g, KD)
                nc.vector.tensor_copy(carry[:, :], state[:, :, GT - 1]).then_inc(carried, 1)

            def finish(g, rows, tiles):
                for t in tiles:
                    wait(dve, ffn3, TILES, g, t + 1)
                    nc.vector.scalar_tensor_tensor(rows[:, t, :], bank[Y3_BANK[t]][:, :], ffn_scale[:, :],
                                                   rows[:, t, :], ALU.mult, ALU.add).then_inc(added3, 1)

            def input_stats(g, parity):
                if isinstance(g, int):
                    dve.wait_ge(loaded_x[parity], 16 * (g // 2 + 1))
                else:
                    dve.wait_ge(loaded_x[parity], 8 * (g - parity) + 16)
                for t in range(TILES):
                    row_stats(0, g, t, x_rows[parity])
                row_moments(0, g)

            input_stats(0, 0)

            def step(s, m, a, b, c, n):
                ga, gb, gc = s, s - 1, s - 2
                rows_a, rows_c = res[m], res[(m - 2) % UNROLL]
                if a:
                    wait(dve, logits1, 2, ga, 0)
                    for k in range(KD):
                        split_lo(n1_hi, KD, N1_T, ga, k, n1h[:, k, :], n1l[:, k, :], n1_lo)
                if b:
                    gate_input(gb, 0)
                if c:
                    add_and_stats(2, gc, Y_T, y_t, added2, rows_c, rows_c, None)
                if a:
                    tree(ga, gate1, prob1, leaf1, tanh1, tree1, leaf1_t)
                if b:
                    gate_input(gb, 1)
                if c:
                    wait(dve, logits3, 2, gc, 0)
                    for k in range(KD):
                        split_lo(n3_hi, KD, N3_T, gc, k, n3h[:, k, :], n3l[:, k, :], n3_lo)
                if n:
                    input_stats(s + 1, (m + 1) % 2)
                if b:
                    gate_input(gb, 2)
                if a:
                    wait(dve, ffn1, TILES, ga, 0)
                    for k in range(KL):
                        split_lo(leaf1_hi, KL, LEAF1_T, ga, k, leaf1h[:, k, :], leaf1l[:, k, :], leaf1_lo)
                if c:
                    tree(gc, gate3, prob3, leaf3, tanh3, tree3, leaf3_t)
                if a:
                    wait(dve, stored[m], 32 // UNROLL, s - m, 0)
                    add_and_stats(1, ga, Y1, ffn1, added1, x_rows[m % 2], rows_a, ffn_scale[:, :])
                if c:
                    wait(dve, ffn3, TILES, gc, 0)
                    for k in range(KL):
                        split_lo(leaf3_hi, KL, LEAF3_T, gc, k, leaf3h[:, k, :], leaf3l[:, k, :], leaf3_lo)
                if b:
                    gate_input(gb, 3)
                if c:
                    finish(gc, rows_c, (0, 1))
                if a:
                    wait(dve, i_out, KD, ga - 2, KD)
                    for k in range(KD):
                        split_lo(n2_hi, KD, N2_T, ga, k, n2h[m % 2][:, k, :], n2l[m % 2][:, k, :], n2_lo)
                if b:
                    scan(gb, (m - 1) % PER_SEQ == 0)
                if c:
                    finish(gc, rows_c, (2, 3))

            steps(dve, step)

        @block.tensor
        def _(pe):
            pe.wait_ge(setup_dve, DVE_SIGN)
            pe.wait_ge(loaded_w, 16 * LOADS)
            nc.tensor.matmul(bank[0][:, 0:1], sign_row[:, :], one[:, :], start=True, stop=True)\
              .then_inc(setup_pe, 1)
            pe.wait_ge(setup_pool, 3)
            pe.wait_ge(setup_dve, DVE_SIGN_READ)
            for k in range(KD):
                ch = slice(k * P, k * P + P)
                nc.tensor.transpose(bank[k][:, 0:P], routers_s[:, 0, ch], ident[:, :])
                nc.tensor.transpose(bank[k][:, P:NODES], routers_s[0:NODES - P, 1, ch],
                                    ident[0:NODES - P, 0:NODES - P])
                nc.tensor.transpose(bank[KD + k][:, 0:P], even_s[:, ch], ident[:, :])
                last = nc.tensor.transpose(bank[KD + k][:, P:LEAVES], odd_s[:, ch], ident[:, :])
            last.then_inc(setup_pe, 1)
            pe.wait_ge(setup_dve, DVE_T1)
            for k in range(KD):
                for j in range(KD):
                    last = nc.tensor.transpose(bank[k][:, j * P:j * P + P], wout_s[:, j, k * P:k * P + P],
                                               ident[:, :])
            last.then_inc(setup_pe, 1)
            for j in range(KD):
                for k in range(KD):
                    last = nc.tensor.matmul(bank[KD + j][:, 0:LEAVES], wq_s[:, k, j * P:j * P + P],
                                            routers_t[:, k, :], start=(k == 0), stop=(k == KD - 1))
            last.then_inc(setup_pe, 1)
            pe.wait_ge(setup_dve, DVE_T2)
            for j in range(KL):
                for k in range(KD):
                    last = nc.tensor.matmul(bank[j][:, :], leaves_t[:, k, j * P:j * P + P],
                                            wout_t[:, k, :], start=(k == 0), stop=(k == KD - 1))
            last.then_inc(setup_pe, 1)
            pe.wait_ge(weights_ready, 1)

            def products(out_, early, late, lo_ready):
                n = len(early) + len(late)
                last = None
                for q, (l, r) in enumerate(early + late):
                    if q == len(early):
                        lo_ready()
                    last = nc.tensor.matmul(out_, l, r, start=(q == 0), stop=(q == n - 1))
                return last

            def transposes_to_channels(g, base, rows, ready, done_sem, free):
                for k in range(KD):
                    free(k)
                    if k == 0:
                        wait(pe, ready, TILES, g, TILES)
                    for t in range(TILES):
                        last = nc.tensor.transpose(bank[(base + k) % BANKS][:, t * P:t * P + P],
                                                   rows[:, t, k * P:k * P + P], ident[:, :])
                    last.then_inc(done_sem, 1)

            def tree_logits(g, base, nh, nl, hi, lo, done_sem, free):
                for j in range(2):
                    free(j)
                    wait(pe, hi, KD, g, KD)
                    for h in range(2):
                        tok = slice((2 * j + h) * P, (2 * j + h + 1) * P)
                        last = products(
                            bank[(base + j) % BANKS][:, h * LEAVES:(h + 1) * LEAVES],
                            [(nh[:, k, tok], w[:, k, :]) for k in range(KD) for w in (w1h, w1l)],
                            [(nl[:, k, tok], w1h[:, k, :]) for k in range(KD)],
                            lambda: wait(pe, lo, KD, g, KD))
                    last.then_inc(done_sem, 1)

            def leaf_transposes(g, base, leaf, tree_sem, done_sem, free):
                for k in range(KL):
                    free(k)
                    wait(pe, tree_sem, TREE, g, TREE - 1 + k)
                    for t in range(TILES):
                        last = nc.tensor.transpose(bank[(base + k) % BANKS][:, t * P:t * P + P],
                                                   leaf[:, t, k * P:k * P + P], ident[:, :])
                    last.then_inc(done_sem, 1)

            def ffn_out(g, banks, lh, ll, hi, lo, done_sem, tiles, free):
                for t in tiles:
                    free(t)
                    wait(pe, hi, KL, g, KL)
                    tok = slice(t * P, t * P + P)
                    products(bank[banks[t]][:, :],
                             [(lh[:, k, tok], w[:, k, :]) for k in range(KL) for w in (w2h, w2l)],
                             [(ll[:, k, tok], w2h[:, k, :]) for k in range(KL)],
                             lambda: wait(pe, lo, KL, g, KL)).then_inc(done_sem, 1)

            def gate(g, par, c, banks, wh, wl, done_sem, free):
                free()
                wait(pe, n2_hi, KD, g, KD)
                ch = slice(c * P, c * P + P)
                nh, nl = n2h[par], n2l[par]
                products(bank[banks[c]][:, :],
                         [(w[:, k, ch], nh[:, k, :]) for k in range(KD) for w in (wh, wl)],
                         [(wh[:, k, ch], nl[:, k, :]) for k in range(KD)],
                         lambda: wait(pe, n2_lo, KD, g, KD)).then_inc(done_sem, 1)

            def y_transposes(g, free):
                for t in range(TILES):
                    free(t)
                    if t == 0:
                        wait(pe, scanned, KD, g, KD)
                    for c in range(KD):
                        last = nc.tensor.transpose(bank[(Y_T + t) % BANKS][:, c * P:c * P + P],
                                                   state[:, c, t * P:t * P + P], ident[:, :])
                    last.then_inc(y_t, 1)

            def step(s, m, a, b, c, n):
                ga, gb, gc = s, s - 1, s - 2

                def free(job):
                    before, step_ = job - BANKS, s
                    while True:
                        if before < 0:
                            before, step_ = before + JOBS, step_ - 1
                        role, release, per, k = RELEASES[before]
                        g = step_ - role
                        if not isinstance(g, int) or 0 <= g < GROUPS:
                            wait(pe, release, per, g, k + 1)
                            return
                        if step_ < 0:
                            return
                        before -= BANKS

                def gates_r(k):
                    gate(gb, (m - 1) % 2, k, R_BANK, wah, wal, r_out, lambda: free(R_JOB[k]))

                def gates_i(k):
                    gate(gb, (m - 1) % 2, k, I_BANK, wxh, wxl, i_out, lambda: free(I_JOB[k]))

                if a:
                    transposes_to_channels(ga, N1_T, norm1, normed[0], n1_t, lambda k: free(N1_T + k))
                if b:
                    gates_r(0)
                    gates_i(0)
                if c:
                    y_transposes(gc, lambda t: free(Y_T + t))
                if a:
                    tree_logits(ga, LOGITS1, n1h, n1l, n1_hi, n1_lo, logits1, lambda j: free(LOGITS1 + j))
                if b:
                    gates_r(1)
                    gates_i(1)
                if c:
                    transposes_to_channels(gc, N3_T, norm3, normed[2], n3_t, lambda k: free(N3_T + k))
                if b:
                    gates_r(2)
                    gates_i(2)
                if a:
                    leaf_transposes(ga, LEAF1_T, leaf1, tree1, leaf1_t, lambda k: free(LEAF1_T + k))
                if c:
                    tree_logits(gc, LOGITS3, n3h, n3l, n3_hi, n3_lo, logits3, lambda j: free(LOGITS3 + j))
                if a:
                    ffn_out(ga, Y1_BANK, leaf1h, leaf1l, leaf1_hi, leaf1_lo, ffn1, range(TILES),
                            lambda t: free(Y1 + t))
                if b:
                    gates_r(3)
                if c:
                    leaf_transposes(gc, LEAF3_T, leaf3, tree3, leaf3_t, lambda k: free(LEAF3_T + k))
                if b:
                    gates_i(3)
                if c:
                    ffn_out(gc, Y3_BANK, leaf3h, leaf3l, leaf3_hi, leaf3_lo, ffn3, (0, 1),
                            lambda t: free(Y3_JOB[t]))
                if a:
                    transposes_to_channels(ga, N2_T, norm2, normed[1], n2_t, lambda k: free(N2_T + k))
                if c:
                    ffn_out(gc, Y3_BANK, leaf3h, leaf3l, leaf3_hi, leaf3_lo, ffn3, (2, 3),
                            lambda t: free(Y3_JOB[t]))

            steps(pe, step)


_INS = ['L0_attn_x', 'L0_attn_Wa', 'L0_attn_Wx', 'L0_attn_ba', 'L0_attn_bx', 'L0_attn_Lam',
        'L0_ffn_Wq', 'L0_ffn_routers', 'L0_ffn_leaf_values', 'L0_ffn_Wout_w', 'L0_ffn_Wout_b']


def kernel(**inputs):
    import concourse.bacc as bacc
    from concourse.bass_utils import run_bass_kernel_spmd

    nc = bacc.Bacc("TRN2", target_bir_lowering=False, num_devices=1)
    arrays, args = {}, []
    for name in _INS:
        a = np.ascontiguousarray(inputs[name])
        arrays[f"in_{name}"] = a
        args.append(nc.dram_tensor(f"in_{name}", a.shape, mybir.dt.from_np(a.dtype), kind="ExternalInput").ap())
    x = arrays["in_L0_attn_x"]
    args.append(nc.dram_tensor("out_x", x.shape, mybir.dt.from_np(x.dtype), kind="ExternalOutput").ap())
    macaron_kernel(nc, *args)
    r = run_bass_kernel_spmd(nc, [arrays], core_ids=[0])
    return r.results[0]["out_x"]
```

```python
import numpy as np
import concourse.bass as bass
from concourse import mybir
from contextlib import ExitStack


def macaron_kernel(
    nc: bass.Bass,
    x_in: bass.AP,
    w_a: bass.AP,
    w_x: bass.AP,
    b_a: bass.AP,
    b_x: bass.AP,
    lam: bass.AP,
    w_q: bass.AP,
    routers: bass.AP,
    leaf_values: bass.AP,
    w_out: bass.AP,
    b_out: bass.AP,
    out: bass.AP,
):
    fp32, fp16, i32, u32 = mybir.dt.float32, mybir.dt.float16, mybir.dt.int32, mybir.dt.uint32
    ALU = mybir.AluOpType
    ACT = mybir.ActivationFunctionType
    AX = mybir.AxisListType
    RMAX = bass.bass_isa.ReduceOp.max

    P = 128
    B, T, D = x_in.shape
    NODES = routers.shape[0]
    LEAVES = leaf_values.shape[0]
    HALF = LEAVES // 2
    DEPTH = LEAVES.bit_length() - 1
    KD = D // P
    KL = LEAVES // P
    GT = 512
    TILES = GT // P
    GROUPS = B * T // GT
    PER_SEQ = T // GT
    BANKS = 8
    SQ = 32
    QUADS = P // SQ
    MOVED = 16 * QUADS * QUADS
    UNROLL = 4
    P_LAST, LAST_G = GROUPS - 2, GROUPS - 1
    FIRST, LOOPS = 4, (GROUPS - 4) // UNROLL - 1
    LAST = FIRST + UNROLL * LOOPS
    assert D == GT and NODES == LEAVES - 1 and KL == 2 and UNROLL % PER_SEQ == 0

    EPS = 1e-5
    LOG_C = float(np.log(8.0))
    XN = 2.0 ** 8
    ROOT = 2.0 ** 7
    HIDDEN_SCALE = ROOT * 2.0 ** (DEPTH - 1)
    TOP = 14
    EXPONENT = 0x7F800000
    ROOT_SCALE = (0.5 / XN) ** 2

    LOGITS1, Y_T, N3_T, LEAF1_T, LOGITS3, Y1, LEAF3_T, Y3, N2_T = 0, 4, 12, 18, 20, 22, 27, 32, 36
    R_JOB, I_JOB = [2, 10, 17, 26], [8, 11, 16, 29]
    JOBS = 40
    LEAF3_T_LATE = 26
    R_BANK, I_BANK = ([j % BANKS for j in jobs] for jobs in (R_JOB, I_JOB))
    assert JOBS % BANKS == 0

    x_g = x_in.rearrange("b t d -> (b t) d").rearrange("(g t p) d -> g p t d", t=TILES, p=P)
    out_g = out.rearrange("b t d -> (b t) d").rearrange("(g t p) d -> g p t d", t=TILES, p=P)

    ctx = ExitStack()
    with ctx:
        def sb(name, shape, dt=fp32):
            return ctx.enter_context(nc.sbuf_tensor(name, shape, dt))

        def sem(name):
            return ctx.enter_context(nc.semaphore(name))

        bank = [ctx.enter_context(nc.psum_tensor(f"bank{i}", [P, 512], fp32)) for i in range(BANKS)]

        x_rows = [sb(f"x_rows{i}", [P, TILES, D]) for i in range(2)]
        res = [sb(f"res{i}", [P, TILES, D]) for i in range(UNROLL)]
        norm1 = sb("norm1", [P, TILES, D])
        norm2 = sb("norm2", [P, TILES, D])
        norm3 = sb("norm3", [P, TILES, D])
        squares = sb("squares", [P, QUADS, KD, TILES * SQ])
        cols1 = norm1[:, :, :].rearrange("p q (k n) -> p q k n", k=KD)
        n1h, n1l = sb("n1h", [P, KD, GT], fp16), sb("n1l", [P, KD, GT], fp16)
        n3h, n3l = sb("n3h", [P, KD, GT], fp16), sb("n3l", [P, KD, GT], fp16)
        n2h = [sb(f"n2h{i}", [P, KD, GT], fp16) for i in range(2)]
        n2l = [sb(f"n2l{i}", [P, KD, GT], fp16) for i in range(2)]
        n2f = sb("n2f", [P, KD, GT])
        gate1, gate3 = sb("gate1", [P, TILES, LEAVES]), sb("gate3", [P, TILES, LEAVES])
        prob1, prob3 = sb("prob1", [P, TILES, HALF]), sb("prob3", [P, TILES, HALF])
        leaf1, leaf3 = sb("leaf1", [P, TILES, LEAVES]), sb("leaf3", [P, TILES, LEAVES])
        leaf1h, leaf1l = sb("leaf1h", [P, KL, GT], fp16), sb("leaf1l", [P, KL, GT], fp16)
        leaf3h, leaf3l = sb("leaf3h", [P, KL, GT], fp16), sb("leaf3l", [P, KL, GT], fp16)
        tanh_r = [sb(f"tanh_r{i}", [P, GT]) for i in range(2)]
        tanh_i = [sb(f"tanh_i{i}", [P, GT]) for i in range(2)]
        decay = sb("decay", [P, KD, GT])
        root = sb("root", [P, KD, GT])
        state = sb("state", [P, KD, GT])
        carry = sb("carry", [P, KD])

        wah, wal = sb("wah", [P, KD, D], fp16), sb("wal", [P, KD, D], fp16)
        wxh, wxl = sb("wxh", [P, KD, D], fp16), sb("wxl", [P, KD, D], fp16)
        w1h, w1l = sb("w1h", [P, KD, LEAVES], fp16), sb("w1l", [P, KD, LEAVES], fp16)
        w2h, w2l = sb("w2h", [P, KL, D], fp16), sb("w2l", [P, KL, D], fp16)

        ident = sb("ident", [P, P])
        minus_half = sb("minus_half", [P, TILES])
        stats = [sb(f"stats{n}", [P, TILES, nc.vector.BN_STATS_DIM]) for n in (1, 2, 3)]
        moments = [sb(f"moments{n}", [P, TILES, nc.vector.BN_AGGR_DIM]) for n in (1, 2, 3)]
        var_eps = [sb(f"var_eps{n}", [P, TILES]) for n in (1, 2, 3)]
        rstd = [sb(f"rstd{n}", [P, TILES]) for n in (1, 2, 3)]
        neg_mean = [sb(f"neg_mean{n}", [P, TILES]) for n in (1, 2, 3)]
        ba_half, bx_half = sb("ba_half", [P, KD]), sb("bx_half", [P, KD])
        lam_col, log_a = sb("lam_col", [P, KD]), sb("log_a", [P, KD])
        lam_abs, lam_exp, lam_ln = sb("lam_abs", [P, KD]), sb("lam_exp", [P, KD]), sb("lam_ln", [P, KD])
        sign_row, one = sb("sign_row", [1, P]), sb("one", [1, 1])
        sign = sb("sign", [P, 1])
        peak_1 = sb("peak_1", [P, 2])
        peak, peak_all, w_scale, w_inv, act_scale = (sb(n, [P, 4]) for n in (
            "peak", "peak_all", "w_scale", "w_inv", "act_scale"))
        W_A, W_X, W_1, W_2 = range(4)
        ffn_scale, root_bias = sb("ffn_scale", [P, 1]), sb("root_bias", [P, 1])

        wq_s, wout_s, wout_t = res[0], res[1], res[2]
        routers_t = res[3][:, 0:2, :].rearrange("p a n -> p (a n)").rearrange("p (k n) -> p k n", k=KD)
        leaves_t = res[3][:, 2:4, :].rearrange("p a n -> p (a n)").rearrange("p (k n) -> p k n", k=KD)
        routers_s = root[:, 0:2, :]
        even_s, odd_s = root[:, 2, :], root[:, 3, :]
        wa_s, wx_s = decay, state
        w2_s = norm3[:, 2:4, :]
        bias_s = norm2[:, 0, :]

        loaded_routers, loaded_wq, loaded_leaves, loaded_wout, loaded_bias, loaded_gates, loaded_cols = map(
            sem, ("loaded_routers", "loaded_wq", "loaded_leaves", "loaded_wout", "loaded_bias",
                  "loaded_gate_weights", "loaded_columns"))
        loaded_x = [sem("loaded_x0"), sem("loaded_x1")]
        stored = [sem(f"stored{i}") for i in range(UNROLL)]
        constants, differences, setup_dve = map(sem, ("constants", "leaf_differences", "setup_dve"))
        sign_made, sign_read, routers_moved = map(sem, ("sign_made", "sign_read", "routers_moved"))
        lam_done, leaves_moved, wout_moved = map(sem, ("lam_done", "leaves_moved", "wout_moved"))
        setup_pe = sem("setup_pe")
        PE_SIGN, PE_ROUTERS, PE_W1, PE_LEAVES, PE_WOUT0, PE_WOUT1, PE_W2 = range(1, 8)
        peaked, peak_known, scale_known, w_hi, w_lo = map(sem, (
            "peaked", "peak_known", "scale_known", "w_hi", "w_lo"))
        W1_PEAK, GATES_PEAK, W2_PEAK = 1, 2, 3
        W1_READY, W2_READY, GATES_READY = 1, 2, 3
        GATE_COLS, W1_COL, W2_COL = slice(W_A, W_X + 1), slice(W_1, W_1 + 1), slice(W_2, W_2 + 1)
        passed = sem("waits_passed")
        n2_t, n3_t = map(sem, ("n2_transposed", "n3_transposed"))
        logits1, logits3 = map(sem, ("logits1", "logits3"))
        leaf1_t, leaf3_t = map(sem, ("leaf1_transposed", "leaf3_transposed"))
        ffn1, ffn3 = map(sem, ("ffn1_out", "ffn3_out"))
        r_out, i_out, y_t = map(sem, ("r_preact", "i_preact", "y_transposed"))
        n1_hi, n2_hi, n3_hi = map(sem, ("n1_hi", "n2_hi", "n3_hi"))
        tanh1, tanh3 = map(sem, ("gates1", "gates3"))
        leaf1_hi, leaf3_hi = map(sem, ("leaf1_hi", "leaf3_hi"))
        r_tanh, i_tanh, decayed, squared, rest = map(sem, (
            "r_tanh", "i_tanh", "decayed", "squared", "one_minus_square"))
        rooted = sem("rooted")
        n2_lo, n3_lo = map(sem, ("n2_lo", "n3_lo"))
        squared_up = sem("squares_transposed")
        leaf1_lo, leaf3_lo = map(sem, ("leaf1_lo", "leaf3_lo"))
        added1, added2, added3 = map(sem, ("added1", "added2", "added3"))
        stat = [sem(f"stat{n}") for n in (1, 2, 3)]
        moment = [sem(f"moment{n}") for n in (1, 2, 3)]
        tree1, tree3 = sem("tree1"), sem("tree3")
        gated, scaled, scanned = map(sem, ("gated", "scaled", "scanned"))
        carried = sem("carried")
        moved = sem("squares_moved")
        n1_lo = sem("n1_lo")
        row_scale = [sem(f"row_scale{n}") for n in (1, 2, 3)]
        normed = [sem(f"normed{n}") for n in (1, 2, 3)]
        TREE = 2 * (DEPTH - 1) + 1

        RELEASES = [None] * JOBS
        for lag, jobs, release in (
                (1, R_JOB, r_tanh), (1, I_JOB, i_tanh),
                (2, range(Y_T, Y_T + TILES), added2), (0, range(LOGITS1, LOGITS1 + 2), tanh1),
                (2, range(N3_T, N3_T + KD), n3_lo), (0, range(LEAF1_T, LEAF1_T + KL), leaf1_lo),
                (2, range(LOGITS3, LOGITS3 + 2), tanh3), (0, range(Y1, Y1 + TILES), added1),
                (2, range(LEAF3_T, LEAF3_T + KL), leaf3_lo), (2, range(Y3, Y3 + TILES), added3),
                (0, range(N2_T, N2_T + KD), n2_lo)):
            for k, job in enumerate(jobs):
                assert RELEASES[job] is None
                RELEASES[job] = (lag, release, len(jobs), k)

        def by_token(k):
            return cols1[:, :, k, :].rearrange("p q (t j) -> p t q j", t=TILES)

        def split_view(columns):
            return columns.rearrange("p (t q j) -> p t q j", q=QUADS, t=TILES)

        block = ctx.enter_context(nc.Block())

        def wait(eng, semaphore, per_group, g, k):
            if isinstance(g, int) and (g < 0 or per_group * g + k <= 0):
                return
            eng.wait_ge(semaphore, per_group * g + k)

        def pass_waits(eng):
            eng.sem_inc(passed, 1)

        def steps(eng, emit):
            def at(s):
                emit(s, s % UNROLL, 1 <= s, 2 <= s, s + 1 < GROUPS)
            for s in range(FIRST):
                at(s)
            with eng.Fori(0, LOOPS) as i:
                for k in range(UNROLL):
                    emit(UNROLL * i + (FIRST + k), (FIRST + k) % UNROLL, True, True, True)
            for s in range(LAST, GROUPS):
                at(s)

        @block.sync
        def _(sp):
            sp.dma_start(routers_s[:, 0, :], routers[0:P, :]).then_inc(loaded_routers, 16)
            sp.dma_start(routers_s[0:NODES - P, 1, :], routers[P:NODES, :]).then_inc(loaded_routers, 16)
            sp.dma_start(x_rows[0][:, :, :], x_g[0, :, :, :]).then_inc(loaded_x[0], 16)
            sp.dma_start(wout_s[:, :, :], w_out.rearrange("(k p) d -> p k d", p=P)).then_inc(loaded_wout, 16)
            sp.dma_start(wx_s[:, :, :], w_x.rearrange("(k p) h -> p k h", p=P)).then_inc(loaded_gates, 16)
            sp.dma_start(x_rows[1][:, :, :], x_g[1, :, :, :]).then_inc(loaded_x[1], 16)

            def move_squares(g):
                wait(sp, squared_up, TILES, g, TILES)
                wait(sp, n1_lo, KD, g, 0)
                for q in range(QUADS):
                    for r in range(QUADS):
                        sp.dma_start(cols1[r * SQ:(r + 1) * SQ, q, :, :],
                                     squares[q * SQ:(q + 1) * SQ, r, :, :]).then_inc(moved, 16)

            def load(g, parity):
                wait(sp, added1, TILES, g - 2, TILES)
                sp.dma_start(x_rows[parity][:, :, :], x_g[g, :, :, :]).then_inc(loaded_x[parity], 16)

            def store(g, slot):
                for h in range(2):
                    wait(sp, added3, TILES, g, 2 * h + 2)
                    sp.dma_start(out_g[g, :, 2 * h:2 * h + 2, :], res[slot][:, 2 * h:2 * h + 2, :])\
                      .then_inc(stored[slot], 16)

            move_squares(0)

            def step(s, m, b, c, n):
                if n:
                    move_squares(s + 1)
                if not isinstance(s, int) or s + 2 < GROUPS:
                    load(s + 2, m % 2)
                if c:
                    store(s - 2, (m - 2) % UNROLL)

            steps(sp, step)
            store(P_LAST, P_LAST % UNROLL)
            store(LAST_G, LAST_G % UNROLL)
            for slot in range(UNROLL):
                sp.wait_ge(stored[slot], 32 * (GROUPS // UNROLL))

        @block.gpsimd
        def _(pool):
            nc.gpsimd.memset(ident[:, :], 0.0).then_inc(constants, 1)
            nc.gpsimd.memset(minus_half[:, :], -0.5).then_inc(constants, 1)
            pool.wait_ge(constants, 2)
            nc.gpsimd.affine_select(out=ident[:, :], in_=ident[:, :], compare_op=ALU.not_equal, fill=1.0,
                                    base=0, pattern=[[-1, P]], channel_multiplier=1).then_inc(constants, 1)
            pool.wait_ge(loaded_leaves, 32)
            nc.gpsimd.tensor_tensor(odd_s, odd_s, even_s, ALU.subtract).then_inc(differences, 1)

            def normalise(n, rows, g, into, free):
                mv = moments[n]
                wait(pool, moment[n], TILES, g, TILES)
                wait(pool, normed[n], TILES, g, 0)
                pass_waits(pool)
                nc.gpsimd.tensor_scalar(var_eps[n][:, :], mv[:, :, 1], XN ** -2, EPS * XN ** -2,
                                        ALU.mult, ALU.add).then_inc(row_scale[n], 1)
                nc.gpsimd.tensor_scalar(neg_mean[n][:, :], mv[:, :, 0], -1.0, 0.0,
                                        ALU.mult, ALU.add).then_inc(row_scale[n], 1)
                wait(pool, row_scale[n], 3, g, 2)
                nc.gpsimd.tensor_tensor(rstd[n][:, :], var_eps[n][:, :], minus_half[:, :],
                                        ALU.pow).then_inc(row_scale[n], 1)
                wait(pool, row_scale[n], 3, g, 3)
                wait(pool, free, KD, g, 0)
                pass_waits(pool)
                for t in range(TILES):
                    nc.gpsimd.tensor_scalar(into[:, t, :], rows[:, t, :], neg_mean[n][:, t:t + 1],
                                            rstd[n][:, t:t + 1], ALU.add, ALU.mult).then_inc(normed[n], 1)

            def overall_peak(count, cols):
                pool.wait_ge(peaked, count)
                nc.gpsimd.partition_all_reduce(peak_all[:, cols], peak[:, cols], P, RMAX)\
                  .then_inc(peak_known, 1)

            def columns_lo(g):
                wait(pool, logits1, 2, g, 0)
                for k in range(KD):
                    wait(pool, n1_hi, KD, g, k + 1)
                    nc.gpsimd.tensor_tensor(split_view(n1l[:, k, :]), by_token(k),
                                            split_view(n1h[:, k, :]), ALU.subtract).then_inc(n1_lo, 1)

            normalise(0, x_rows[0], 0, norm1, n1_lo)
            overall_peak(W1_PEAK, W1_COL)
            overall_peak(GATES_PEAK, GATE_COLS)
            columns_lo(0)
            overall_peak(W2_PEAK, W2_COL)

            def step(s, m, b, c, n):
                if n:
                    normalise(0, x_rows[(m + 1) % 2], s + 1, norm1, n1_lo)
                if c:
                    normalise(2, res[(m - 2) % UNROLL], s - 2, norm3, n3_t)
                head = isinstance(s, int) and s == 0
                if n and not head:
                    columns_lo(s + 1)
                normalise(1, res[m], s, norm2, n2_t)
                if head:
                    columns_lo(s + 1)

            steps(pool, step)
            normalise(2, res[P_LAST % UNROLL], P_LAST, norm3, n3_t)
            normalise(2, res[LAST_G % UNROLL], LAST_G, norm3, n3_t)

        @block.scalar
        def _(act):
            act.dma_start(wq_s[:, :, :], w_q.rearrange("(k p) d -> p k d", p=P)).then_inc(loaded_wq, 16)
            halves = leaf_values.rearrange("(k two) d -> two k d", two=2)
            act.dma_start(even_s, halves[0, :, :]).then_inc(loaded_leaves, 16)
            act.dma_start(odd_s, halves[1, :, :]).then_inc(loaded_leaves, 16)
            act.dma_start(bias_s, b_out.rearrange("(a d) -> a d", a=1).to_broadcast([P, D]))\
               .then_inc(loaded_bias, 16)
            with nc.allow_non_contiguous_dma(reason="512 biases by channel, once"):
                for col, vec in ((ba_half, b_a), (bx_half, b_x), (lam_col, lam)):
                    act.dma_start(col[:, :], vec.rearrange("(c p) -> p c", p=P)).then_inc(loaded_cols, 16)
            act.dma_start(wa_s[:, :, :], w_a.rearrange("(k p) h -> p k h", p=P)).then_inc(loaded_gates, 16)
            act.wait_ge(setup_pe, PE_LEAVES)
            for j in range(2):
                nc.scalar.activation(leaves_t[:, 2 * j:2 * j + 2, :].rearrange("p k n -> p (k n)"),
                                     bank[4 + j][:, :], ACT.Copy).then_inc(leaves_moved, 1)
            for k in range(KD):
                act.wait_ge(setup_pe, (PE_WOUT0, PE_WOUT1)[k // 2])
                nc.scalar.activation(wout_t[:, k, :], bank[2 + k][:, :], ACT.Copy).then_inc(wout_moved, 1)
            act.wait_ge(loaded_cols, 48)
            nc.scalar.activation(lam_abs[:, :], lam_col[:, :], ACT.Abs).then_inc(lam_done, 1)
            act.wait_ge(lam_done, 1)
            nc.scalar.activation(lam_exp[:, :], lam_abs[:, :], ACT.Exp, scale=-1.0).then_inc(lam_done, 1)
            act.wait_ge(lam_done, 2)
            nc.scalar.activation(lam_ln[:, :], lam_exp[:, :], ACT.Ln, bias=1.0).then_inc(lam_done, 1)

            def weights_hi(ready, parts):
                act.wait_ge(scale_known, ready)
                for hi, w, j in parts:
                    last = nc.scalar.activation(hi, w, ACT.Copy, scale=w_scale[:, j:j + 1])
                last.then_inc(w_hi, 1)

            weights_hi(W1_READY, [(w1h[:, 2 * j:2 * j + 2, :].rearrange("p k n -> p (k n)"),
                                   bank[6 + j][:, :], W_1) for j in range(2)])

            def split_hi(src_sem, per, base, g, k, hi, hi_sem):
                wait(act, src_sem, per, g, k + 1)
                nc.scalar.activation(hi, bank[(base + k) % BANKS][:, :], ACT.Copy).then_inc(hi_sem, 1)

            def r_gate(g, c):
                wait(act, r_out, KD, g, c + 1)
                wait(act, decayed, KD, g, c - 1)
                nc.scalar.activation(tanh_r[c % 2][:, :], bank[R_BANK[c]][:, :], ACT.Tanh,
                                     bias=ba_half[:, c:c + 1],
                                     scale=act_scale[:, W_A:W_A + 1]).then_inc(r_tanh, 1)

            def r_decay(g, c):
                wait(act, r_tanh, KD, g, c + 1)
                wait(act, scanned, KD, g - 1, c + 1)
                nc.scalar.activation(decay[:, c, :], tanh_r[c % 2][:, :], ACT.Exp,
                                     bias=log_a[:, c:c + 1], scale=-0.5 * LOG_C).then_inc(decayed, 1)

            def r_root(g, c):
                wait(act, decayed, KD, g, c + 1)
                wait(act, scaled, KD, g - 1, c + 1)
                nc.scalar.activation(root[:, c, :], decay[:, c, :], ACT.Square).then_inc(squared, 1)
                wait(act, squared, KD, g, c + 1)
                nc.scalar.activation(root[:, c, :], root[:, c, :], ACT.Relu, scale=-ROOT_SCALE,
                                     bias=root_bias[:, :]).then_inc(rest, 1)

            def i_gate(g, c):
                wait(act, i_out, KD, g, c + 1)
                wait(act, gated, KD, g, c - 1)
                nc.scalar.activation(tanh_i[c % 2][:, :], bank[I_BANK[c]][:, :], ACT.Tanh,
                                     bias=bx_half[:, c:c + 1],
                                     scale=act_scale[:, W_X:W_X + 1]).then_inc(i_tanh, 1)

            def tree_gates(g, j, logits, base, gates, tanhs, tree):
                wait(act, logits, 2, g, j + 1)
                wait(act, tree, TREE, g, 0)
                nc.scalar.activation(gates[:, 2 * j:2 * j + 2, :].rearrange("p t n -> p (t n)"),
                                     bank[(base + j) % BANKS][:, :], ACT.Tanh,
                                     scale=act_scale[:, W_1:W_1 + 1]).then_inc(tanhs, 1)

            def columns_hi(g):
                wait(act, logits1, 2, g, 0)
                wait(act, moved, MOVED, g, MOVED)
                for k in range(KD):
                    nc.scalar.activation(split_view(n1h[:, k, :]), by_token(k), ACT.Copy)\
                      .then_inc(n1_hi, 1)

            def columns3_hi(g):
                wait(act, logits3, 2, g, 0)
                for k in range(KD):
                    split_hi(n3_t, KD, N3_T, g, k, n3h[:, k, :], n3_hi)

            def leaves3_hi(g, base):
                wait(act, ffn3, TILES, g, 0)
                for k in range(KL):
                    split_hi(leaf3_t, KL, base, g, k, leaf3h[:, k, :], leaf3_hi)

            def gates3(g):
                for j in range(2):
                    tree_gates(g, j, logits3, LOGITS3, gate3, tanh3, tree3)

            def gates_and_decay(g, c):
                r_gate(g, c)
                i_gate(g, c)
                r_decay(g, c)
                r_root(g, c)

            def take_roots(g):
                wait(act, rest, KD, g, KD)
                nc.scalar.activation(root[:, :, :], root[:, :, :], ACT.Sqrt).then_inc(rooted, 1)

            columns_hi(0)

            def step(s, m, b, c, n):
                ga, gb, gc = s, s - 1, s - 2
                head = isinstance(s, int) and s == 0
                if head:
                    weights_hi(W2_READY, [(w2h[:, :, :], w2_s, W_2)])
                for j in range(2):
                    tree_gates(ga, j, logits1, LOGITS1, gate1, tanh1, tree1)
                if b:
                    gates_and_decay(gb, 0)
                if head:
                    weights_hi(GATES_READY, [(wah[:, :, :], wa_s[:, :, :], W_A),
                                             (wxh[:, :, :], wx_s[:, :, :], W_X)])
                if b:
                    gates_and_decay(gb, 1)
                if c:
                    columns3_hi(gc)
                if b:
                    gates_and_decay(gb, 2)
                wait(act, ffn1, TILES, ga, 0)
                for k in range(KL):
                    split_hi(leaf1_t, KL, LEAF1_T, ga, k, leaf1h[:, k, :], leaf1_hi)
                if c:
                    gates3(gc)
                if n:
                    columns_hi(ga + 1)
                if b:
                    r_gate(gb, 3)
                    r_decay(gb, 3)
                if c:
                    leaves3_hi(gc, LEAF3_T)
                if b:
                    r_root(gb, 3)
                    i_gate(gb, 3)
                    take_roots(gb)
                wait(act, gated, KD, gb, KD)
                wait(act, i_out, KD, ga - 2, KD)
                for k in range(KD):
                    wait(act, n2_t, KD, ga, k + 1)
                    nc.scalar.activation(n2f[:, k, :], bank[(N2_T + k) % BANKS][:, :], ACT.Copy)
                    nc.scalar.activation(n2h[m % 2][:, k, :], bank[(N2_T + k) % BANKS][:, :],
                                         ACT.Copy).then_inc(n2_hi, 1)

            steps(act, step)
            for c in range(KD - 1):
                gates_and_decay(LAST_G, c)
            columns3_hi(P_LAST)
            gates_and_decay(LAST_G, KD - 1)
            take_roots(LAST_G)
            gates3(P_LAST)
            columns3_hi(LAST_G)
            leaves3_hi(P_LAST, LEAF3_T_LATE)
            gates3(LAST_G)
            leaves3_hi(LAST_G, LEAF3_T)

        @block.vector
        def _(dve):
            done = [0]

            def link(ins):
                done[0] += 1
                ins.then_inc(setup_dve, 1)
                dve.wait_ge(setup_dve, done[0])

            nc.vector.memset(one[:, :], 1.0)
            nc.vector.memset(root_bias[:, :], ROOT_SCALE)
            nc.vector.memset(carry[:, :], 0.0)
            link(nc.vector.memset(sign_row[:, :], 1.0))
            for bit in range(DEPTH - 1):
                left = sign_row[0:1, :].rearrange("o (h two l) -> o h two l", two=2, l=2 ** bit)[:, :, 0, :]
                ins = nc.vector.tensor_scalar(left, left, -1.0, None, ALU.mult)
                if bit < DEPTH - 2:
                    link(ins)
            ins.then_inc(sign_made, 1)
            dve.wait_ge(setup_pe, PE_SIGN)
            nc.vector.tensor_copy(sign[:, :], bank[7][:, 0:1]).then_inc(sign_read, 1)
            nc.vector.memset(routers_t[:, :, NODES:LEAVES], 0.0).then_inc(routers_moved, 1)
            dve.wait_ge(setup_pe, PE_ROUTERS)
            for k in range(KD):
                nc.vector.tensor_copy(routers_t[:, k, 0:NODES], bank[k][:, 0:NODES]).then_inc(routers_moved, 1)

            def split_lo(hi_sem, per, base, g, k, hi, lo, lo_sem):
                wait(dve, hi_sem, per, g, k + 1)
                nc.vector.tensor_tensor(lo, bank[(base + k) % BANKS][:, :], hi, ALU.subtract)\
                  .then_inc(lo_sem, 1)

            def row_stats(n, g, t, rows):
                nc.vector.bn_stats(stats[n][:, t, :], rows[:, t, :]).then_inc(stat[n], 1)

            def row_moments(n, g):
                wait(dve, normed[n], TILES, g, 0)
                wait(dve, stat[n], TILES, g, TILES)
                pass_waits(dve)
                for t in range(TILES):
                    nc.vector.bn_aggr(moments[n][:, t, :], stats[n][:, t, :]).then_inc(moment[n], 1)

            def add_and_stats(n, g, base, ffn, added, rows_in, rows, scale):
                for t in range(TILES):
                    wait(dve, ffn, TILES, g, t + 1)
                    src = bank[(base + t) % BANKS][:, :]
                    if scale is None:
                        nc.vector.tensor_tensor(rows[:, t, :], src, rows_in[:, t, :], ALU.add).then_inc(added, 1)
                    else:
                        nc.vector.scalar_tensor_tensor(rows[:, t, :], src, scale, rows_in[:, t, :],
                                                       ALU.mult, ALU.add).then_inc(added, 1)
                    if t:
                        wait(dve, added, TILES, g, t)
                        row_stats(n, g, t - 1, rows)
                wait(dve, added, TILES, g, TILES)
                row_stats(n, g, TILES - 1, rows)
                row_moments(n, g)

            def tree(g, gates, probs, leaf, tanhs, tree_sem, leaf_t):
                wait(dve, tanhs, 2, g, 2)
                count = 0
                for level in range(DEPTH - 1):
                    n = 2 ** level
                    t = gates[:, :, n - 1:2 * n - 1]
                    if level:
                        wait(dve, tree_sem, TREE, g, count)
                    if level == DEPTH - 2:
                        wait(dve, leaf_t, KL, g, 0)
                        under = leaf[:, :, 0:HALF]
                    else:
                        under = probs[:, :, 2 * n:4 * n]
                    under = under.rearrange("p t (n two) -> p t n two", two=2)
                    for side, sign_of in ((1, 1.0), (0, -1.0)):
                        if level == 0:
                            nc.vector.tensor_scalar(under[:, :, :, side], t, sign_of, ROOT, ALU.add, ALU.mult)\
                              .then_inc(tree_sem, 1)
                        else:
                            nc.vector.scalar_tensor_tensor(under[:, :, :, side], t, sign_of,
                                                           probs[:, :, n:2 * n], ALU.add, ALU.mult)\
                              .then_inc(tree_sem, 1)
                        count += 1
                wait(dve, tree_sem, TREE, g, count)
                nc.vector.scalar_tensor_tensor(leaf[:, :, HALF:LEAVES], gates[:, :, HALF - 1:NODES], 1.0,
                                               leaf[:, :, 0:HALF], ALU.add, ALU.mult).then_inc(tree_sem, 1)

            def gate_input(g, c):
                wait(dve, i_tanh, KD, g, c + 1)
                if c == 0:
                    wait(dve, y_t, TILES, g, 0)
                nc.vector.scalar_tensor_tensor(state[:, c, :], tanh_i[c % 2][:, :], 1.0, n2f[:, c, :],
                                               ALU.add, ALU.mult).then_inc(gated, 1)

            def scale_input(g, c):
                if c == 0:
                    wait(dve, rooted, 1, g, 1)
                wait(dve, gated, KD, g, c + 1)
                nc.vector.tensor_tensor(state[:, c, :], state[:, c, :], root[:, c, :], ALU.mult)\
                  .then_inc(scaled, 1)

            def scan(g, first):
                if not first:
                    wait(dve, carried, 1, g, 0)
                for c in range(KD):
                    wait(dve, scaled, KD, g, c + 1)
                    nc.vector.tensor_tensor_scan(state[:, c, :], decay[:, c, :], state[:, c, :],
                                                 0.0 if first else carry[:, c:c + 1],
                                                 ALU.mult, ALU.add).then_inc(scanned, 1)
                wait(dve, scanned, KD, g, KD)
                nc.vector.tensor_copy(carry[:, :], state[:, :, GT - 1]).then_inc(carried, 1)

            def finish(g, rows):
                for t in range(TILES):
                    wait(dve, ffn3, TILES, g, t + 1)
                    nc.vector.scalar_tensor_tensor(rows[:, t, :], bank[(Y3 + t) % BANKS][:, :],
                                                   ffn_scale[:, :], rows[:, t, :],
                                                   ALU.mult, ALU.add).then_inc(added3, 1)

            def input_stats(g, parity):
                if isinstance(g, int):
                    dve.wait_ge(loaded_x[parity], 16 * (g // 2 + 1))
                else:
                    dve.wait_ge(loaded_x[parity], 8 * (g - parity) + 16)
                for t in range(TILES):
                    row_stats(0, g, t, x_rows[parity])
                row_moments(0, g)

            def transpose_squares(g):
                for t in range(TILES):
                    wait(dve, normed[0], TILES, g, t + 1)
                    if t == 0:
                        wait(dve, moved, MOVED, g, 0)
                    nc.vector.transpose(
                        squares[:, :, :, t * SQ:(t + 1) * SQ].rearrange("p r k j -> p k r j").bitcast(u32),
                        norm1[:, t, :].rearrange("p (k r j) -> p k r j", r=QUADS, j=SQ).bitcast(u32))\
                      .then_inc(squared_up, 1)

            input_stats(0, 0)
            dve.wait_ge(loaded_cols, 48)
            nc.vector.tensor_scalar(ba_half[:, :], ba_half[:, :], 0.5, None, ALU.mult)
            nc.vector.tensor_scalar(bx_half[:, :], bx_half[:, :], 0.5, None, ALU.mult)

            def set_scale(peak_count, cols):
                dve.wait_ge(peak_known, peak_count)
                link(nc.vector.tensor_scalar(peak_all[:, cols], peak_all[:, cols], 2.0 ** -96, 2.0 ** 96,
                                             ALU.max, ALU.min))
                link(nc.vector.tensor_scalar(w_inv[:, cols].bitcast(i32), peak_all[:, cols].bitcast(i32),
                                             EXPONENT, None, ALU.bitwise_and))
                link(nc.vector.tensor_scalar(w_scale[:, cols].bitcast(i32), w_inv[:, cols].bitcast(i32),
                                             EXPONENT, None, ALU.bitwise_xor))
                link(nc.vector.tensor_scalar(w_scale[:, cols], w_scale[:, cols], 2.0 ** (TOP - 1), None,
                                             ALU.mult))
                link(nc.vector.tensor_scalar(w_inv[:, cols], w_inv[:, cols], 2.0 ** -TOP, None, ALU.mult))
                nc.vector.tensor_scalar(act_scale[:, cols], w_inv[:, cols], 0.5 / XN, None, ALU.mult)\
                  .then_inc(scale_known, 1)

            def weights_lo(ready, parts):
                dve.wait_ge(w_hi, ready)
                for lo, w, hi, j in parts:
                    last = nc.vector.scalar_tensor_tensor(lo, w, w_scale[:, j:j + 1], hi,
                                                          ALU.mult, ALU.subtract)
                last.then_inc(w_lo, 1)

            def flat(t, j):
                return t[:, 2 * j:2 * j + 2, :].rearrange("p k n -> p (k n)")

            transpose_squares(0)
            dve.wait_ge(setup_pe, PE_W1)
            for j in range(2):
                link(nc.vector.reduce_max(peak_1[:, j:j + 1], bank[6 + j][:, :], AX.X,
                                          apply_absolute_value=True))
            nc.vector.tensor_tensor(peak[:, W_1:W_1 + 1], peak_1[:, 0:1], peak_1[:, 1:2], ALU.max)\
              .then_inc(peaked, 1)
            set_scale(W1_PEAK, W1_COL)
            weights_lo(W1_READY, [(flat(w1l, j), bank[6 + j][:, :], flat(w1h, j), W_1) for j in range(2)])
            dve.wait_ge(loaded_gates, 32)
            nc.vector.reduce_max(peak[:, W_A:W_A + 1], wa_s[:, :, :], AX.XY, apply_absolute_value=True)
            nc.vector.reduce_max(peak[:, W_X:W_X + 1], wx_s[:, :, :], AX.XY, apply_absolute_value=True)\
              .then_inc(peaked, 1)

            def combine_w2():
                dve.wait_ge(setup_pe, PE_W2)
                dve.wait_ge(loaded_bias, 16)
                link(nc.vector.tensor_tensor(w2_s[:, 0, :], bank[4][:, :], bias_s, ALU.add))
                link(nc.vector.tensor_scalar(w2_s[:, 0, :], w2_s[:, 0, :], sign[:, :], 2.0,
                                             ALU.mult, ALU.mult))
                link(nc.vector.tensor_scalar(w2_s[:, 1, :], bank[5][:, :], sign[:, :], None, ALU.mult))
                nc.vector.reduce_max(peak[:, W_2:W_2 + 1], w2_s, AX.XY, apply_absolute_value=True)\
                  .then_inc(peaked, 1)
                set_scale(W2_PEAK, W2_COL)
                link(nc.vector.tensor_scalar(ffn_scale[:, :], w_inv[:, W2_COL],
                                             0.5 / (2.0 * HIDDEN_SCALE), None, ALU.mult))
                set_scale(GATES_PEAK, GATE_COLS)

            def decay_bias():
                dve.wait_ge(lam_done, 3)
                link(nc.vector.scalar_tensor_tensor(log_a[:, :], lam_col[:, :], 0.0, lam_ln[:, :],
                                                    ALU.min, ALU.subtract))
                link(nc.vector.tensor_scalar(log_a[:, :], log_a[:, :], -0.5 * LOG_C, None, ALU.add))

            def columns3_lo(g):
                wait(dve, logits3, 2, g, 0)
                for k in range(KD):
                    split_lo(n3_hi, KD, N3_T, g, k, n3h[:, k, :], n3l[:, k, :], n3_lo)

            def leaves3_lo(g, base):
                wait(dve, ffn3, TILES, g, 0)
                for k in range(KL):
                    split_lo(leaf3_hi, KL, base, g, k, leaf3h[:, k, :], leaf3l[:, k, :], leaf3_lo)

            def step(s, m, b, c, n):
                ga, gb, gc = s, s - 1, s - 2
                rows_a, rows_c = res[m], res[(m - 2) % UNROLL]
                head = isinstance(s, int) and s == 0
                if head:
                    combine_w2()
                if n:
                    input_stats(s + 1, (m + 1) % 2)
                if c:
                    add_and_stats(2, gc, Y_T, y_t, added2, rows_c, rows_c, None)
                tree(ga, gate1, prob1, leaf1, tanh1, tree1, leaf1_t)
                if head:
                    weights_lo(W2_READY, [(w2l[:, :, :], w2_s, w2h[:, :, :], W_2)])
                if n:
                    transpose_squares(s + 1)
                if b:
                    gate_input(gb, 0)
                    gate_input(gb, 1)
                if c:
                    columns3_lo(gc)
                if b:
                    gate_input(gb, 2)
                wait(dve, ffn1, TILES, ga, 0)
                for k in range(KL):
                    split_lo(leaf1_hi, KL, LEAF1_T, ga, k, leaf1h[:, k, :], leaf1l[:, k, :], leaf1_lo)
                if c:
                    tree(gc, gate3, prob3, leaf3, tanh3, tree3, leaf3_t)
                wait(dve, stored[m], 32 // UNROLL, s - m, 0)
                add_and_stats(1, ga, Y1, ffn1, added1, x_rows[m % 2], rows_a, ffn_scale[:, :])
                if head:
                    weights_lo(GATES_READY, [(wal[:, :, :], wa_s[:, :, :], wah[:, :, :], W_A),
                                             (wxl[:, :, :], wx_s[:, :, :], wxh[:, :, :], W_X)])
                    decay_bias()
                if c:
                    leaves3_lo(gc, LEAF3_T)
                if b:
                    gate_input(gb, 3)
                if c:
                    finish(gc, rows_c)
                wait(dve, i_out, KD, ga - 2, KD)
                for k in range(KD):
                    if b:
                        scale_input(gb, k)
                    split_lo(n2_hi, KD, N2_T, ga, k, n2h[m % 2][:, k, :], n2l[m % 2][:, k, :], n2_lo)
                if b:
                    scan(gb, (m - 1) % PER_SEQ == 0)

            steps(dve, step)
            rows_p, rows_l = res[P_LAST % UNROLL], res[LAST_G % UNROLL]
            add_and_stats(2, P_LAST, Y_T, y_t, added2, rows_p, rows_p, None)
            for c in range(KD - 1):
                gate_input(LAST_G, c)
            columns3_lo(P_LAST)
            gate_input(LAST_G, KD - 1)
            for c in range(KD):
                scale_input(LAST_G, c)
            scan(LAST_G, LAST_G % PER_SEQ == 0)
            add_and_stats(2, LAST_G, Y_T, y_t, added2, rows_l, rows_l, None)
            tree(P_LAST, gate3, prob3, leaf3, tanh3, tree3, leaf3_t)
            columns3_lo(LAST_G)
            leaves3_lo(P_LAST, LEAF3_T_LATE)
            tree(LAST_G, gate3, prob3, leaf3, tanh3, tree3, leaf3_t)
            finish(P_LAST, rows_p)
            leaves3_lo(LAST_G, LEAF3_T)
            finish(LAST_G, rows_l)

        @block.tensor
        def _(pe):
            pe.wait_ge(sign_made, 1)
            nc.tensor.matmul(bank[7][:, 0:1], sign_row[:, :], one[:, :], start=True, stop=True)\
              .then_inc(setup_pe, 1)
            pe.wait_ge(constants, 3)
            pe.wait_ge(loaded_routers, 32)
            for k in range(KD):
                ch = slice(k * P, k * P + P)
                nc.tensor.transpose(bank[k][:, 0:P], routers_s[:, 0, ch], ident[:, :])
                last = nc.tensor.transpose(bank[k][:, P:NODES], routers_s[0:NODES - P, 1, ch],
                                           ident[0:NODES - P, 0:NODES - P])
            last.then_inc(setup_pe, 1)
            pe.wait_ge(routers_moved, 1 + KD)
            pe.wait_ge(loaded_wq, 16)
            pe.wait_ge(sign_read, 1)
            for j in range(KD):
                for k in range(KD):
                    last = nc.tensor.matmul(bank[6 + j // 2][:, j % 2 * LEAVES:(j % 2 + 1) * LEAVES],
                                            wq_s[:, k, j * P:j * P + P], routers_t[:, k, :],
                                            start=(k == 0), stop=(k == KD - 1))
            last.then_inc(setup_pe, 1)
            pe.wait_ge(differences, 1)
            for k in range(KD):
                ch, at_ = slice(k * P, k * P + P), k % 2 * LEAVES
                nc.tensor.transpose(bank[4 + k // 2][:, at_:at_ + P], even_s[:, ch], ident[:, :])
                last = nc.tensor.transpose(bank[4 + k // 2][:, at_ + P:at_ + LEAVES], odd_s[:, ch], ident[:, :])
            last.then_inc(setup_pe, 1)
            pe.wait_ge(loaded_wout, 16)
            for k in range(KD):
                if k == 2:
                    pe.wait_ge(leaves_moved, 2)
                for j in range(KD):
                    last = nc.tensor.transpose(bank[2 + k][:, j * P:j * P + P],
                                               wout_s[:, j, k * P:k * P + P], ident[:, :])
                if k % 2:
                    last.then_inc(setup_pe, 1)
            pe.wait_ge(wout_moved, KD)
            for j in range(KL):
                for k in range(KD):
                    last = nc.tensor.matmul(bank[4 + j][:, :], leaves_t[:, k, j * P:j * P + P],
                                            wout_t[:, k, :], start=(k == 0), stop=(k == KD - 1))
            last.then_inc(setup_pe, 1)

            def products(out_, early, late, lo_ready, hi_ready=None):
                n = len(early) + len(late)
                last = None
                for q, (l, r) in enumerate(early + late):
                    if q >= len(early):
                        lo_ready(q - len(early))
                    elif hi_ready and q % 2 == 0:
                        hi_ready(q // 2)
                    last = nc.tensor.matmul(out_, l, r, start=(q == 0), stop=(q == n - 1))
                return last

            def by_chunk(semaphore, chunks, g, first=True):
                def ready(k):
                    if first or k == 0:
                        wait(pe, semaphore, chunks, g, k + 1 if first else chunks)
                return ready

            def transposes_to_channels(g, base, rows, ready, done_sem, free):
                for k in range(KD):
                    free(k)
                    if k == 0:
                        wait(pe, ready, TILES, g, TILES)
                    for t in range(TILES):
                        last = nc.tensor.transpose(bank[(base + k) % BANKS][:, t * P:t * P + P],
                                                   rows[:, t, k * P:k * P + P], ident[:, :])
                    last.then_inc(done_sem, 1)

            def tree_logits(g, base, nh, nl, hi, lo, done_sem, free):
                for j in range(2):
                    free(j)
                    for h in range(2):
                        tok = slice((2 * j + h) * P, (2 * j + h + 1) * P)
                        last = products(
                            bank[(base + j) % BANKS][:, h * LEAVES:(h + 1) * LEAVES],
                            [(nh[:, k, tok], w[:, k, :]) for k in range(KD) for w in (w1h, w1l)],
                            [(nl[:, k, tok], w1h[:, k, :]) for k in range(KD)],
                            by_chunk(lo, KD, g, j == h == 0), by_chunk(hi, KD, g, True) if j == h == 0 else None)
                    last.then_inc(done_sem, 1)

            def leaf_transposes(g, base, leaf, tree_sem, done_sem, free):
                for k in range(KL):
                    free(k)
                    wait(pe, tree_sem, TREE, g, TREE - 1 + k)
                    for t in range(TILES):
                        last = nc.tensor.transpose(bank[(base + k) % BANKS][:, t * P:t * P + P],
                                                   leaf[:, t, k * P:k * P + P], ident[:, :])
                    last.then_inc(done_sem, 1)

            def ffn_out(g, base, lh, ll, hi, lo, done_sem, free):
                for t in range(TILES):
                    free(t)
                    tok = slice(t * P, t * P + P)
                    products(bank[(base + t) % BANKS][:, :],
                             [(lh[:, k, tok], w[:, k, :]) for k in range(KL) for w in (w2h, w2l)],
                             [(ll[:, k, tok], w2h[:, k, :]) for k in range(KL)],
                             by_chunk(lo, KL, g, t == 0),
                             by_chunk(hi, KL, g) if t == 0 else None).then_inc(done_sem, 1)

            user = {}

            def free(s, job, place=None):
                lag, release, per, k = RELEASES[job]
                at_ = (place or job) % BANKS
                before = user.get(at_)
                user[at_] = (release, per, s - lag, k)
                if isinstance(s, int):
                    if before:
                        wait(pe, before[0], before[1], before[2], before[3] + 1)
                    return
                before = job - BANKS
                while RELEASES[before % JOBS] is None:
                    before -= BANKS
                lag, release, per, k = RELEASES[before % JOBS]
                wait(pe, release, per, s - lag if before >= 0 else s - 1 - lag, k + 1)

            def first_logits(g, s):
                tree_logits(g, LOGITS1, n1h, n1l, n1_hi, n1_lo, logits1, lambda j: free(s, LOGITS1 + j))

            def r_gate(g, par, c, s):
                gate(g, par, c, R_JOB, wah, wal, r_out, s)

            def i_gate(g, par, c, s):
                gate(g, par, c, I_JOB, wxh, wxl, i_out, s)

            def gates(g, par, c, s):
                r_gate(g, par, c, s)
                i_gate(g, par, c, s)

            def gate(g, par, c, jobs, wh, wl, done_sem, s):
                free(s, jobs[c])
                ch = slice(c * P, c * P + P)
                nh, nl = n2h[par], n2l[par]
                first = done_sem is r_out and c == 0
                products(bank[jobs[c] % BANKS][:, :],
                         [(w[:, k, ch], nh[:, k, :]) for k in range(KD) for w in (wh, wl)],
                         [(wh[:, k, ch], nl[:, k, :]) for k in range(KD)],
                         by_chunk(n2_lo, KD, g, first), by_chunk(n2_hi, KD, g) if first else None)\
                    .then_inc(done_sem, 1)

            def y_transposes(g, s):
                for t in range(TILES):
                    free(s, Y_T + t)
                    if t == 0:
                        wait(pe, scanned, KD, g, KD)
                    for c in range(KD):
                        last = nc.tensor.transpose(bank[(Y_T + t) % BANKS][:, c * P:c * P + P],
                                                   state[:, c, t * P:t * P + P], ident[:, :])
                    last.then_inc(y_t, 1)

            def normed3_columns(g, s):
                transposes_to_channels(g, N3_T, norm3, normed[2], n3_t, lambda k: free(s, N3_T + k))

            def logits_3(g, s):
                tree_logits(g, LOGITS3, n3h, n3l, n3_hi, n3_lo, logits3, lambda j: free(s, LOGITS3 + j))

            def leaves_3(g, base, s):
                leaf_transposes(g, base, leaf3, tree3, leaf3_t,
                                lambda k: free(s, LEAF3_T + k, base + k))

            def ffn_3(g, s):
                ffn_out(g, Y3, leaf3h, leaf3l, leaf3_hi, leaf3_lo, ffn3, lambda t: free(s, Y3 + t))

            def step(s, m, b, c, n):
                ga, gb, gc = s, s - 1, s - 2
                par = (m - 1) % 2
                head = isinstance(s, int) and s == 0
                if head:
                    pe.wait_ge(w_lo, W1_READY)
                first_logits(ga, s)
                if isinstance(s, int) and s == 1:
                    pe.wait_ge(w_lo, GATES_READY)
                if b:
                    r_gate(gb, par, 0, s)
                if c:
                    y_transposes(gc, s)
                if b:
                    i_gate(gb, par, 0, s)
                if b:
                    r_gate(gb, par, 1, s)
                    i_gate(gb, par, 1, s)
                    r_gate(gb, par, 2, s)
                if c:
                    normed3_columns(gc, s)
                if b:
                    i_gate(gb, par, 2, s)
                leaf_transposes(ga, LEAF1_T, leaf1, tree1, leaf1_t, lambda k: free(s, LEAF1_T + k))
                if c:
                    logits_3(gc, s)
                if head:
                    pe.wait_ge(w_lo, W2_READY)
                ffn_out(ga, Y1, leaf1h, leaf1l, leaf1_hi, leaf1_lo, ffn1, lambda t: free(s, Y1 + t))
                if b:
                    r_gate(gb, par, 3, s)
                if c:
                    leaves_3(gc, LEAF3_T, s)
                if b:
                    i_gate(gb, par, 3, s)
                if c:
                    ffn_3(gc, s)
                transposes_to_channels(ga, N2_T, norm2, normed[1], n2_t, lambda k: free(s, N2_T + k))

            steps(pe, step)
            s_p, s_l, par = GROUPS, GROUPS + 1, LAST_G % 2
            gates(LAST_G, par, 0, s_p)
            y_transposes(P_LAST, s_p)
            gates(LAST_G, par, 1, s_p)
            gates(LAST_G, par, 2, s_p)
            normed3_columns(P_LAST, s_p)
            gates(LAST_G, par, 3, s_p)
            logits_3(P_LAST, s_p)
            y_transposes(LAST_G, s_l)
            normed3_columns(LAST_G, s_l)
            leaves_3(P_LAST, LEAF3_T_LATE, s_p)
            logits_3(LAST_G, s_l)
            ffn_3(P_LAST, s_p)
            leaves_3(LAST_G, LEAF3_T, s_l)
            ffn_3(LAST_G, s_l)


_INS = ['L0_attn_x', 'L0_attn_Wa', 'L0_attn_Wx', 'L0_attn_ba', 'L0_attn_bx', 'L0_attn_Lam',
        'L0_ffn_Wq', 'L0_ffn_routers', 'L0_ffn_leaf_values', 'L0_ffn_Wout_w', 'L0_ffn_Wout_b']


def kernel(**inputs):
    import concourse.bacc as bacc
    from concourse.bass_utils import run_bass_kernel_spmd

    nc = bacc.Bacc("TRN2", target_bir_lowering=False, num_devices=1)
    arrays, args = {}, []
    for name in _INS:
        a = np.ascontiguousarray(inputs[name])
        arrays[f"in_{name}"] = a
        args.append(nc.dram_tensor(f"in_{name}", a.shape, mybir.dt.from_np(a.dtype), kind="ExternalInput").ap())
    x = arrays["in_L0_attn_x"]
    args.append(nc.dram_tensor("out_x", x.shape, mybir.dt.from_np(x.dtype), kind="ExternalOutput").ap())
    macaron_kernel(nc, *args)
    r = run_bass_kernel_spmd(nc, [arrays], core_ids=[0])
    return r.results[0]["out_x"]
```

```python
import numpy as np
import concourse.bass as bass
from concourse import mybir
from contextlib import ExitStack


def macaron_kernel(
    nc: bass.Bass,
    x_in: bass.AP,
    w_a: bass.AP,
    w_x: bass.AP,
    b_a: bass.AP,
    b_x: bass.AP,
    lam: bass.AP,
    w_q: bass.AP,
    routers: bass.AP,
    leaf_values: bass.AP,
    w_out: bass.AP,
    b_out: bass.AP,
    out: bass.AP,
):
    fp32, fp16, i32, u32 = mybir.dt.float32, mybir.dt.float16, mybir.dt.int32, mybir.dt.uint32
    ALU = mybir.AluOpType
    ACT = mybir.ActivationFunctionType
    AX = mybir.AxisListType
    RMAX = bass.bass_isa.ReduceOp.max

    P = 128
    B, T, D = x_in.shape
    NODES = routers.shape[0]
    LEAVES = leaf_values.shape[0]
    HALF = LEAVES // 2
    DEPTH = LEAVES.bit_length() - 1
    KD = D // P
    KL = LEAVES // P
    GT = 512
    TILES = GT // P
    GROUPS = B * T // GT
    PER_SEQ = T // GT
    BANKS = 8
    SQ = 32
    QUADS = P // SQ
    MOVED = 16 * QUADS * QUADS
    UNROLL = 4
    D_LAST, P_LAST, LAST_G = GROUPS - 3, GROUPS - 2, GROUPS - 1
    FIRST, LOOPS = 4, (GROUPS - 4) // UNROLL - 1
    LAST = FIRST + UNROLL * LOOPS
    assert D == GT and NODES == LEAVES - 1 and KL == 2 and UNROLL % PER_SEQ == 0

    EPS = 1e-5
    LOG_C = float(np.log(8.0))
    XN = 2.0 ** 8
    ROOT = 2.0 ** 7
    HIDDEN_SCALE = ROOT * 2.0 ** (DEPTH - 1)
    TOP = 14
    EXPONENT = 0x7F800000
    ROOT_SCALE = (0.5 / XN) ** 2

    LOGITS1, Y_T, LOGITS3, LEAF1_T, Y1, LEAF3_T, Y3 = 0, 2, 6, 8, 14, 24, 28
    R_JOB, I_JOB = [10, 12, 18, 20], [11, 13, 19, 21]
    JOBS = 32
    N3_T = 36
    R_BANK, I_BANK = ([j % BANKS for j in jobs] for jobs in (R_JOB, I_JOB))
    assert JOBS % BANKS == 0

    x_g = x_in.rearrange("b t d -> (b t) d").rearrange("(g t p) d -> g p t d", t=TILES, p=P)
    out_g = out.rearrange("b t d -> (b t) d").rearrange("(g t p) d -> g p t d", t=TILES, p=P)

    ctx = ExitStack()
    with ctx:
        def sb(name, shape, dt=fp32):
            return ctx.enter_context(nc.sbuf_tensor(name, shape, dt))

        def sem(name):
            return ctx.enter_context(nc.semaphore(name))

        bank = [ctx.enter_context(nc.psum_tensor(f"bank{i}", [P, 512], fp32)) for i in range(BANKS)]

        x_rows = [sb(f"x_rows{i}", [P, TILES, D]) for i in range(2)]
        res = [sb(f"res{i}", [P, TILES, D]) for i in range(UNROLL)]
        norm1 = sb("norm1", [P, TILES, D])
        norm2 = sb("norm2", [P, TILES, D])
        norm3 = sb("norm3", [P, TILES, D])
        squares, squares_b = (sb(n, [P, QUADS, KD, TILES * SQ]) for n in ("squares", "squares_b"))
        cols2 = sb("cols2", [P, QUADS, KD, TILES * SQ])
        cols1, cols3 = (n[:, :, :].rearrange("p q (k n) -> p q k n", k=KD) for n in (norm1, norm3))
        n1h, n1l = sb("n1h", [P, KD, GT], fp16), sb("n1l", [P, KD, GT], fp16)
        n3h, n3l = sb("n3h", [P, KD, GT], fp16), sb("n3l", [P, KD, GT], fp16)
        n2h, n2l = sb("n2h", [P, KD, GT], fp16), sb("n2l", [P, KD, GT], fp16)
        gate1, gate3 = sb("gate1", [P, TILES, LEAVES]), sb("gate3", [P, TILES, LEAVES])
        prob1, prob3 = sb("prob1", [P, TILES, HALF]), sb("prob3", [P, TILES, HALF])
        leaf1, leaf3 = sb("leaf1", [P, TILES, LEAVES]), sb("leaf3", [P, TILES, LEAVES])
        leaf1h, leaf1l = sb("leaf1h", [P, KL, GT], fp16), sb("leaf1l", [P, KL, GT], fp16)
        leaf3h, leaf3l = sb("leaf3h", [P, KL, GT], fp16), sb("leaf3l", [P, KL, GT], fp16)
        tanh_r = [sb(f"tanh_r{i}", [P, GT]) for i in range(2)]
        tanh_i = [sb(f"tanh_i{i}", [P, GT]) for i in range(2)]
        decay = sb("decay", [P, KD, GT])
        root = sb("root", [P, KD, GT])
        state = sb("state", [P, KD, GT])
        carry = sb("carry", [P, KD])

        wah, wal = sb("wah", [P, KD, D], fp16), sb("wal", [P, KD, D], fp16)
        wxh, wxl = sb("wxh", [P, KD, D], fp16), sb("wxl", [P, KD, D], fp16)
        w1h, w1l = sb("w1h", [P, KD, LEAVES], fp16), sb("w1l", [P, KD, LEAVES], fp16)
        w2h, w2l = sb("w2h", [P, KL, D], fp16), sb("w2l", [P, KL, D], fp16)

        ident = sb("ident", [P, P])
        minus_half = sb("minus_half", [P, TILES])
        stats = [sb(f"stats{n}", [P, TILES, nc.vector.BN_STATS_DIM]) for n in (1, 2, 3)]
        moments = [sb(f"moments{n}", [P, TILES, nc.vector.BN_AGGR_DIM]) for n in (1, 2, 3)]
        var_eps = [sb(f"var_eps{n}", [P, TILES]) for n in (1, 2, 3)]
        rstd = [sb(f"rstd{n}", [P, TILES]) for n in (1, 2, 3)]
        neg_mean = [sb(f"neg_mean{n}", [P, TILES]) for n in (1, 2, 3)]
        ba_half, bx_half = sb("ba_half", [P, KD]), sb("bx_half", [P, KD])
        lam_col, log_a = sb("lam_col", [P, KD]), sb("log_a", [P, KD])
        lam_abs, lam_exp, lam_ln = sb("lam_abs", [P, KD]), sb("lam_exp", [P, KD]), sb("lam_ln", [P, KD])
        sign_row, one = sb("sign_row", [1, P]), sb("one", [1, 1])
        sign = sb("sign", [P, 1])
        peak_1 = sb("peak_1", [P, 2])
        peak, peak_all, w_scale, w_inv, act_scale = (sb(n, [P, 4]) for n in (
            "peak", "peak_all", "w_scale", "w_inv", "act_scale"))
        W_A, W_X, W_1, W_2 = range(4)
        ffn_scale, root_bias = sb("ffn_scale", [P, 1]), sb("root_bias", [P, 1])

        wq_s, wout_s, wout_t = res[0], res[1], res[2]
        routers_t = res[3][:, 0:2, :].rearrange("p a n -> p (a n)").rearrange("p (k n) -> p k n", k=KD)
        leaves_t = res[3][:, 2:4, :].rearrange("p a n -> p (a n)").rearrange("p (k n) -> p k n", k=KD)
        routers_s = root[:, 0:2, :]
        even_s, odd_s = root[:, 2, :], root[:, 3, :]
        wa_s, wx_s = decay, state
        w2_s = norm3[:, 2:4, :]
        bias_s = norm2[:, 0, :]

        loaded_routers, loaded_wq, loaded_leaves, loaded_wout, loaded_bias, loaded_gates, loaded_cols = map(
            sem, ("loaded_routers", "loaded_wq", "loaded_leaves", "loaded_wout", "loaded_bias",
                  "loaded_gate_weights", "loaded_columns"))
        loaded_x = [sem("loaded_x0"), sem("loaded_x1")]
        stored = [sem(f"stored{i}") for i in range(UNROLL)]
        constants, differences, setup_dve = map(sem, ("constants", "leaf_differences", "setup_dve"))
        sign_made, sign_read, routers_moved = map(sem, ("sign_made", "sign_read", "routers_moved"))
        lam_done, leaves_moved, wout_moved = map(sem, ("lam_done", "leaves_moved", "wout_moved"))
        setup_pe = sem("setup_pe")
        PE_SIGN, PE_ROUTERS, PE_W1, PE_LEAVES, PE_WOUT0, PE_WOUT1, PE_W2 = range(1, 8)
        peaked, peak_known, scale_known, w_hi, w_lo = map(sem, (
            "peaked", "peak_known", "scale_known", "w_hi", "w_lo"))
        W1_PEAK, GATES_PEAK, W2_PEAK = 1, 2, 3
        W1_READY, W2_READY, GATES_READY = 1, 2, 3
        GATE_COLS, W1_COL, W2_COL = slice(W_A, W_X + 1), slice(W_1, W_1 + 1), slice(W_2, W_2 + 1)
        passed = sem("waits_passed")
        n3_t = sem("n3_transposed")
        logits1, logits3 = map(sem, ("logits1", "logits3"))
        leaf1_t, leaf3_t = map(sem, ("leaf1_transposed", "leaf3_transposed"))
        ffn1, ffn3 = map(sem, ("ffn1_out", "ffn3_out"))
        r_out, i_out, y_t = map(sem, ("r_preact", "i_preact", "y_transposed"))
        n1_hi, n2_hi, n3_hi = map(sem, ("n1_hi", "n2_hi", "n3_hi"))
        tanh1, tanh3 = map(sem, ("gates1", "gates3"))
        leaf1_hi, leaf3_hi = map(sem, ("leaf1_hi", "leaf3_hi"))
        r_tanh, i_tanh, decayed, squared, rest = map(sem, (
            "r_tanh", "i_tanh", "decayed", "squared", "one_minus_square"))
        rooted = sem("rooted")
        squared_up1, squared_up2, squared_up3 = (sem(f"squares{n}_transposed") for n in (1, 2, 3))
        leaf1_lo, leaf3_lo = map(sem, ("leaf1_lo", "leaf3_lo"))
        added1, added2, added3 = map(sem, ("added1", "added2", "added3"))
        stat = [sem(f"stat{n}") for n in (1, 2, 3)]
        moment = [sem(f"moment{n}") for n in (1, 2, 3)]
        tree1, tree3 = sem("tree1"), sem("tree3")
        gated, scaled, scanned = map(sem, ("gated", "scaled", "scanned"))
        carried = sem("carried")
        moved1, moved2, moved3 = (sem(f"squares{n}_moved") for n in (1, 2, 3))
        n1_lo, n2_lo, n3_lo = map(sem, ("n1_lo", "n2_lo", "n3_lo"))
        row_scale = [sem(f"row_scale{n}") for n in (1, 2, 3)]
        normed = [sem(f"normed{n}") for n in (1, 2, 3)]
        TREE = 2 * (DEPTH - 1) + 1

        RELEASES = [None] * (N3_T + KD)
        for lag, jobs, release in (
                (1, R_JOB, r_tanh), (1, I_JOB, i_tanh),
                (2, range(Y_T, Y_T + TILES), added2), (0, range(LOGITS1, LOGITS1 + 2), tanh1),
                (0, range(LEAF1_T, LEAF1_T + KL), leaf1_lo),
                (3, range(LOGITS3, LOGITS3 + 2), tanh3), (0, range(Y1, Y1 + TILES), added1),
                (3, range(LEAF3_T, LEAF3_T + KL), leaf3_lo), (3, range(Y3, Y3 + TILES), added3),
                (2, range(N3_T, N3_T + KD), n3_lo)):
            for k, job in enumerate(jobs):
                assert RELEASES[job] is None
                RELEASES[job] = (lag, release, len(jobs), k)

        def by_token(cols, k):
            return cols[:, :, k, :].rearrange("p q (t j) -> p t q j", t=TILES)

        def split_view(columns):
            return columns.rearrange("p (t q j) -> p t q j", q=QUADS, t=TILES)

        block = ctx.enter_context(nc.Block())

        def wait(eng, semaphore, per_group, g, k):
            if isinstance(g, int) and (g < 0 or per_group * g + k <= 0):
                return
            eng.wait_ge(semaphore, per_group * g + k)

        def pass_waits(eng):
            eng.sem_inc(passed, 1)

        def steps(eng, emit):
            def at(s):
                emit(s, s % UNROLL, 1 <= s, 2 <= s, 3 <= s, s + 1 < GROUPS)
            for s in range(FIRST):
                at(s)
            with eng.Fori(0, LOOPS) as i:
                for k in range(UNROLL):
                    emit(UNROLL * i + (FIRST + k), (FIRST + k) % UNROLL, True, True, True, True)
            for s in range(LAST, GROUPS):
                at(s)

        @block.sync
        def _(sp):
            sp.dma_start(routers_s[:, 0, :], routers[0:P, :]).then_inc(loaded_routers, 16)
            sp.dma_start(routers_s[0:NODES - P, 1, :], routers[P:NODES, :]).then_inc(loaded_routers, 16)
            sp.dma_start(x_rows[0][:, :, :], x_g[0, :, :, :]).then_inc(loaded_x[0], 16)
            sp.dma_start(wout_s[:, :, :], w_out.rearrange("(k p) d -> p k d", p=P)).then_inc(loaded_wout, 16)
            sp.dma_start(wx_s[:, :, :], w_x.rearrange("(k p) h -> p k h", p=P)).then_inc(loaded_gates, 16)
            sp.dma_start(x_rows[1][:, :, :], x_g[1, :, :, :]).then_inc(loaded_x[1], 16)

            def move_squares(g, made, source, split, cols, done_sem):
                wait(sp, made, TILES, g, TILES)
                wait(sp, split, KD, g, 0)
                if cols is cols2:
                    wait(sp, scaled, KD, g, 0)
                for q in range(QUADS):
                    for r in range(QUADS):
                        sp.dma_start(cols[r * SQ:(r + 1) * SQ, q, :, :],
                                     source[q * SQ:(q + 1) * SQ, r, :, :]).then_inc(done_sem, 16)

            def load(g, parity):
                wait(sp, added1, TILES, g - 2, TILES)
                sp.dma_start(x_rows[parity][:, :, :], x_g[g, :, :, :]).then_inc(loaded_x[parity], 16)

            def store(g, slot):
                for h in range(2):
                    wait(sp, added3, TILES, g, 2 * h + 2)
                    sp.dma_start(out_g[g, :, 2 * h:2 * h + 2, :], res[slot][:, 2 * h:2 * h + 2, :])\
                      .then_inc(stored[slot], 16)

            def move1(g):
                move_squares(g, squared_up1, squares, n1_lo, cols1, moved1)

            def move3(g):
                move_squares(g, squared_up3, squares, n3_lo, cols3, moved3)

            move1(0)

            def step(s, m, b, c, d, n):
                if n:
                    move1(s + 1)
                if not isinstance(s, int) or s + 2 < GROUPS:
                    load(s + 2, m % 2)
                if c:
                    move3(s - 2)
                move_squares(s, squared_up2, squares_b, n2_lo, cols2, moved2)
                if d:
                    store(s - 3, (m - 3) % UNROLL)

            steps(sp, step)
            move3(P_LAST)
            for g in (D_LAST, P_LAST, LAST_G):
                store(g, g % UNROLL)
            for slot in range(UNROLL):
                sp.wait_ge(stored[slot], 32 * (GROUPS // UNROLL))

        @block.gpsimd
        def _(pool):
            nc.gpsimd.memset(ident[:, :], 0.0).then_inc(constants, 1)
            nc.gpsimd.memset(minus_half[:, :], -0.5).then_inc(constants, 1)
            pool.wait_ge(constants, 2)
            nc.gpsimd.affine_select(out=ident[:, :], in_=ident[:, :], compare_op=ALU.not_equal, fill=1.0,
                                    base=0, pattern=[[-1, P]], channel_multiplier=1).then_inc(constants, 1)
            pool.wait_ge(loaded_leaves, 32)
            nc.gpsimd.tensor_tensor(odd_s, odd_s, even_s, ALU.subtract).then_inc(differences, 1)

            def normalise(n, rows, g, into, free):
                mv = moments[n]
                wait(pool, moment[n], TILES, g, TILES)
                wait(pool, normed[n], TILES, g, 0)
                pass_waits(pool)
                nc.gpsimd.tensor_scalar(var_eps[n][:, :], mv[:, :, 1], XN ** -2, EPS * XN ** -2,
                                        ALU.mult, ALU.add).then_inc(row_scale[n], 1)
                nc.gpsimd.tensor_scalar(neg_mean[n][:, :], mv[:, :, 0], -1.0, 0.0,
                                        ALU.mult, ALU.add).then_inc(row_scale[n], 1)
                wait(pool, row_scale[n], 3, g, 2)
                nc.gpsimd.tensor_tensor(rstd[n][:, :], var_eps[n][:, :], minus_half[:, :],
                                        ALU.pow).then_inc(row_scale[n], 1)
                wait(pool, row_scale[n], 3, g, 3)
                wait(pool, free, KD, g, 0)
                pass_waits(pool)
                for t in range(TILES):
                    nc.gpsimd.tensor_scalar(into[:, t, :], rows[:, t, :], neg_mean[n][:, t:t + 1],
                                            rstd[n][:, t:t + 1], ALU.add, ALU.mult).then_inc(normed[n], 1)

            def overall_peak(count, cols):
                pool.wait_ge(peaked, count)
                nc.gpsimd.partition_all_reduce(peak_all[:, cols], peak[:, cols], P, RMAX)\
                  .then_inc(peak_known, 1)

            def columns_lo(g, logits, hi_sem, cols, hi, lo, lo_sem):
                if cols is cols2:
                    wait(pool, i_out, KD, g, 0)
                else:
                    wait(pool, logits, 2, g, 0)
                for k in range(KD):
                    wait(pool, hi_sem, KD, g, k + 1)
                    nc.gpsimd.tensor_tensor(split_view(lo[:, k, :]), by_token(cols, k),
                                            split_view(hi[:, k, :]), ALU.subtract).then_inc(lo_sem, 1)

            def columns1_lo(g):
                columns_lo(g, logits1, n1_hi, cols1, n1h, n1l, n1_lo)

            def columns2_lo(g):
                columns_lo(g, None, n2_hi, cols2, n2h, n2l, n2_lo)

            def columns3_lo(g):
                columns_lo(g, logits3, n3_hi, cols3, n3h, n3l, n3_lo)

            normalise(0, x_rows[0], 0, norm1, n1_lo)
            overall_peak(W1_PEAK, W1_COL)
            overall_peak(GATES_PEAK, GATE_COLS)
            columns1_lo(0)
            overall_peak(W2_PEAK, W2_COL)

            def step(s, m, b, c, d, n):
                if n:
                    normalise(0, x_rows[(m + 1) % 2], s + 1, norm1, n1_lo)
                if b:
                    columns2_lo(s - 1)
                if c:
                    normalise(2, res[(m - 2) % UNROLL], s - 2, norm3, n3_lo)
                if n:
                    columns1_lo(s + 1)
                normalise(1, res[m], s, norm2, squared_up2)
                if c:
                    columns3_lo(s - 2)

            steps(pool, step)
            columns2_lo(LAST_G)
            normalise(2, res[P_LAST % UNROLL], P_LAST, norm3, n3_lo)
            columns3_lo(P_LAST)
            normalise(2, res[LAST_G % UNROLL], LAST_G, norm3, n3_lo)

        @block.scalar
        def _(act):
            act.dma_start(wq_s[:, :, :], w_q.rearrange("(k p) d -> p k d", p=P)).then_inc(loaded_wq, 16)
            halves = leaf_values.rearrange("(k two) d -> two k d", two=2)
            act.dma_start(even_s, halves[0, :, :]).then_inc(loaded_leaves, 16)
            act.dma_start(odd_s, halves[1, :, :]).then_inc(loaded_leaves, 16)
            act.dma_start(bias_s, b_out.rearrange("(a d) -> a d", a=1).to_broadcast([P, D]))\
               .then_inc(loaded_bias, 16)
            with nc.allow_non_contiguous_dma(reason="512 biases by channel, once"):
                for col, vec in ((ba_half, b_a), (bx_half, b_x), (lam_col, lam)):
                    act.dma_start(col[:, :], vec.rearrange("(c p) -> p c", p=P)).then_inc(loaded_cols, 16)
            act.dma_start(wa_s[:, :, :], w_a.rearrange("(k p) h -> p k h", p=P)).then_inc(loaded_gates, 16)
            act.wait_ge(setup_pe, PE_LEAVES)
            for j in range(2):
                nc.scalar.activation(leaves_t[:, 2 * j:2 * j + 2, :].rearrange("p k n -> p (k n)"),
                                     bank[4 + j][:, :], ACT.Copy).then_inc(leaves_moved, 1)
            for k in range(KD):
                act.wait_ge(setup_pe, (PE_WOUT0, PE_WOUT1)[k // 2])
                nc.scalar.activation(wout_t[:, k, :], bank[2 + k][:, :], ACT.Copy).then_inc(wout_moved, 1)
            act.wait_ge(loaded_cols, 48)
            nc.scalar.activation(lam_abs[:, :], lam_col[:, :], ACT.Abs).then_inc(lam_done, 1)
            act.wait_ge(lam_done, 1)
            nc.scalar.activation(lam_exp[:, :], lam_abs[:, :], ACT.Exp, scale=-1.0).then_inc(lam_done, 1)
            act.wait_ge(lam_done, 2)
            nc.scalar.activation(lam_ln[:, :], lam_exp[:, :], ACT.Ln, bias=1.0).then_inc(lam_done, 1)

            def weights_hi(ready, parts):
                act.wait_ge(scale_known, ready)
                for hi, w, j in parts:
                    last = nc.scalar.activation(hi, w, ACT.Copy, scale=w_scale[:, j:j + 1])
                last.then_inc(w_hi, 1)

            weights_hi(W1_READY, [(w1h[:, 2 * j:2 * j + 2, :].rearrange("p k n -> p (k n)"),
                                   bank[6 + j][:, :], W_1) for j in range(2)])

            def split_hi(src_sem, per, base, g, k, hi, hi_sem):
                wait(act, src_sem, per, g, k + 1)
                nc.scalar.activation(hi, bank[(base + k) % BANKS][:, :], ACT.Copy).then_inc(hi_sem, 1)

            def r_gate(g, c):
                wait(act, r_out, KD, g, c + 1)
                wait(act, decayed, KD, g, c - 1)
                nc.scalar.activation(tanh_r[c % 2][:, :], bank[R_BANK[c]][:, :], ACT.Tanh,
                                     bias=ba_half[:, c:c + 1],
                                     scale=act_scale[:, W_A:W_A + 1]).then_inc(r_tanh, 1)

            def r_decay(g, c):
                wait(act, r_tanh, KD, g, c + 1)
                wait(act, scanned, KD, g - 1, c + 1)
                nc.scalar.activation(decay[:, c, :], tanh_r[c % 2][:, :], ACT.Exp,
                                     bias=log_a[:, c:c + 1], scale=-0.5 * LOG_C).then_inc(decayed, 1)

            def r_square(g, c):
                wait(act, decayed, KD, g, c + 1)
                wait(act, scaled, KD, g - 1, c + 1)
                nc.scalar.activation(root[:, c, :], decay[:, c, :], ACT.Square).then_inc(squared, 1)

            def r_rest(g, c):
                wait(act, squared, KD, g, c + 1)
                nc.scalar.activation(root[:, c, :], root[:, c, :], ACT.Relu, scale=-ROOT_SCALE,
                                     bias=root_bias[:, :]).then_inc(rest, 1)

            def i_gate(g, c):
                wait(act, i_out, KD, g, c + 1)
                wait(act, gated, KD, g, c - 1)
                nc.scalar.activation(tanh_i[c % 2][:, :].rearrange("p (q t j) -> p t q j", q=QUADS, t=TILES),
                                     split_view(bank[I_BANK[c]][:, :]), ACT.Tanh,
                                     bias=bx_half[:, c:c + 1],
                                     scale=act_scale[:, W_X:W_X + 1]).then_inc(i_tanh, 1)

            def tree_gates(g, j, logits, base, gates, tanhs, tree):
                wait(act, logits, 2, g, j + 1)
                wait(act, tree, TREE, g, 0)
                nc.scalar.activation(gates[:, 2 * j:2 * j + 2, :].rearrange("p t n -> p (t n)"),
                                     bank[(base + j) % BANKS][:, :], ACT.Tanh,
                                     scale=act_scale[:, W_1:W_1 + 1]).then_inc(tanhs, 1)

            def columns_hi(g, logits, moved_sem, cols, hi, hi_sem):
                if cols is cols2:
                    wait(act, i_out, KD, g, 0)
                else:
                    wait(act, logits, 2, g, 0)
                wait(act, moved_sem, MOVED, g, MOVED)
                for k in range(KD):
                    nc.scalar.activation(split_view(hi[:, k, :]), by_token(cols, k), ACT.Copy)\
                      .then_inc(hi_sem, 1)

            def columns1_hi(g):
                columns_hi(g, logits1, moved1, cols1, n1h, n1_hi)

            def columns2_hi(g):
                columns_hi(g, None, moved2, cols2, n2h, n2_hi)

            def columns3_hi(g):
                columns_hi(g, logits3, moved3, cols3, n3h, n3_hi)

            def leaves3_hi(g):
                wait(act, ffn3, TILES, g, 0)
                for k in range(KL):
                    split_hi(leaf3_t, KL, LEAF3_T, g, k, leaf3h[:, k, :], leaf3_hi)

            def gate_1(g, j):
                tree_gates(g, j, logits1, LOGITS1, gate1, tanh1, tree1)

            def gate_3(g, j):
                tree_gates(g, j, logits3, LOGITS3, gate3, tanh3, tree3)

            def gates3(g):
                gate_3(g, 0)
                gate_3(g, 1)

            def gates_and_decay(g, c):
                r_gate(g, c)
                i_gate(g, c)
                r_decay(g, c)
                r_square(g, c)
                r_rest(g, c)

            def take_roots(g):
                wait(act, rest, KD, g, KD)
                nc.scalar.activation(root[:, :, :], root[:, :, :], ACT.Sqrt).then_inc(rooted, 1)

            def last_gates(g):
                r_gate(g, 3)
                r_decay(g, 3)
                r_square(g, 3)
                i_gate(g, 3)
                r_rest(g, 3)
                take_roots(g)

            columns1_hi(0)

            def step(s, m, b, c, d, n):
                ga, gb, gc, gd = s, s - 1, s - 2, s - 3
                head = isinstance(s, int) and s == 0
                if head:
                    weights_hi(W2_READY, [(w2h[:, :, :], w2_s, W_2)])
                gate_1(ga, 0)
                gate_1(ga, 1)
                if d:
                    gate_3(gd, 0)
                wait(act, ffn1, TILES, ga, 0)
                for k in range(KL):
                    split_hi(leaf1_t, KL, LEAF1_T, ga, k, leaf1h[:, k, :], leaf1_hi)
                if head:
                    weights_hi(GATES_READY, [(wah[:, :, :], wa_s[:, :, :], W_A),
                                             (wxh[:, :, :], wx_s[:, :, :], W_X)])
                if d:
                    gate_3(gd, 1)
                if b:
                    columns2_hi(gb)
                    gates_and_decay(gb, 0)
                if n:
                    columns1_hi(ga + 1)
                if b:
                    gates_and_decay(gb, 1)
                    gates_and_decay(gb, 2)
                if d:
                    leaves3_hi(gd)
                if b:
                    last_gates(gb)
                if c:
                    columns3_hi(gc)

            steps(act, step)
            columns2_hi(LAST_G)
            gates3(D_LAST)
            for c in range(KD - 1):
                gates_and_decay(LAST_G, c)
            leaves3_hi(D_LAST)
            last_gates(LAST_G)
            columns3_hi(P_LAST)
            gates3(P_LAST)
            wait(act, logits3, 2, LAST_G, 0)
            for k in range(KD):
                split_hi(n3_t, KD, N3_T, 0, k, n3h[:, k, :], n3_hi)
            leaves3_hi(P_LAST)
            gates3(LAST_G)
            leaves3_hi(LAST_G)

        @block.vector
        def _(dve):
            done = [0]

            def link(ins):
                done[0] += 1
                ins.then_inc(setup_dve, 1)
                dve.wait_ge(setup_dve, done[0])

            nc.vector.memset(one[:, :], 1.0)
            nc.vector.memset(root_bias[:, :], ROOT_SCALE)
            nc.vector.memset(carry[:, :], 0.0)
            link(nc.vector.memset(sign_row[:, :], 1.0))
            for bit in range(DEPTH - 1):
                left = sign_row[0:1, :].rearrange("o (h two l) -> o h two l", two=2, l=2 ** bit)[:, :, 0, :]
                ins = nc.vector.tensor_scalar(left, left, -1.0, None, ALU.mult)
                if bit < DEPTH - 2:
                    link(ins)
            ins.then_inc(sign_made, 1)
            dve.wait_ge(setup_pe, PE_SIGN)
            nc.vector.tensor_copy(sign[:, :], bank[7][:, 0:1]).then_inc(sign_read, 1)
            nc.vector.memset(routers_t[:, :, NODES:LEAVES], 0.0).then_inc(routers_moved, 1)
            dve.wait_ge(setup_pe, PE_ROUTERS)
            for k in range(KD):
                nc.vector.tensor_copy(routers_t[:, k, 0:NODES], bank[k][:, 0:NODES]).then_inc(routers_moved, 1)

            def split_lo(hi_sem, per, base, g, k, hi, lo, lo_sem):
                wait(dve, hi_sem, per, g, k + 1)
                nc.vector.tensor_tensor(lo, bank[(base + k) % BANKS][:, :], hi, ALU.subtract)\
                  .then_inc(lo_sem, 1)

            def row_stats(n, g, t, rows):
                nc.vector.bn_stats(stats[n][:, t, :], rows[:, t, :]).then_inc(stat[n], 1)

            def row_moments(n, g):
                wait(dve, normed[n], TILES, g, 0)
                wait(dve, stat[n], TILES, g, TILES)
                pass_waits(dve)
                for t in range(TILES):
                    nc.vector.bn_aggr(moments[n][:, t, :], stats[n][:, t, :]).then_inc(moment[n], 1)

            def add_and_stats(n, g, base, ffn, added, rows_in, rows, scale):
                for t in range(TILES):
                    wait(dve, ffn, TILES, g, t + 1)
                    src = bank[(base + t) % BANKS][:, :]
                    if scale is None:
                        nc.vector.tensor_tensor(rows[:, t, :], src, rows_in[:, t, :], ALU.add).then_inc(added, 1)
                    else:
                        nc.vector.scalar_tensor_tensor(rows[:, t, :], src, scale, rows_in[:, t, :],
                                                       ALU.mult, ALU.add).then_inc(added, 1)
                    if t:
                        wait(dve, added, TILES, g, t)
                        row_stats(n, g, t - 1, rows)
                wait(dve, added, TILES, g, TILES)
                row_stats(n, g, TILES - 1, rows)
                row_moments(n, g)

            def tree(g, gates, probs, leaf, tanhs, tree_sem, leaf_t):
                wait(dve, tanhs, 2, g, 2)
                count = 0
                for level in range(DEPTH - 1):
                    n = 2 ** level
                    t = gates[:, :, n - 1:2 * n - 1]
                    if level:
                        wait(dve, tree_sem, TREE, g, count)
                    if level == DEPTH - 2:
                        wait(dve, leaf_t, KL, g, 0)
                        under = leaf[:, :, 0:HALF]
                    else:
                        under = probs[:, :, 2 * n:4 * n]
                    under = under.rearrange("p t (n two) -> p t n two", two=2)
                    for side, sign_of in ((1, 1.0), (0, -1.0)):
                        if level == 0:
                            nc.vector.tensor_scalar(under[:, :, :, side], t, sign_of, ROOT, ALU.add, ALU.mult)\
                              .then_inc(tree_sem, 1)
                        else:
                            nc.vector.scalar_tensor_tensor(under[:, :, :, side], t, sign_of,
                                                           probs[:, :, n:2 * n], ALU.add, ALU.mult)\
                              .then_inc(tree_sem, 1)
                        count += 1
                wait(dve, tree_sem, TREE, g, count)
                nc.vector.scalar_tensor_tensor(leaf[:, :, HALF:LEAVES], gates[:, :, HALF - 1:NODES], 1.0,
                                               leaf[:, :, 0:HALF], ALU.add, ALU.mult).then_inc(tree_sem, 1)

            def gate_input(g, c):
                wait(dve, i_tanh, KD, g, c + 1)
                nc.vector.scalar_tensor_tensor(
                    cols2[:, :, c, :], tanh_i[c % 2][:, :].rearrange("p (q n) -> p q n", q=QUADS), 1.0,
                    cols2[:, :, c, :], ALU.add, ALU.mult).then_inc(gated, 1)

            def scale_input(g, c):
                if c == 0:
                    wait(dve, rooted, 1, g, 1)
                    wait(dve, y_t, TILES, g, 0)
                wait(dve, gated, KD, g, c + 1)
                nc.vector.tensor_tensor(split_view(state[:, c, :]), by_token(cols2, c),
                                        split_view(root[:, c, :]), ALU.mult).then_inc(scaled, 1)

            def scan(g, first):
                if not first:
                    wait(dve, carried, 1, g, 0)
                for c in range(KD):
                    wait(dve, scaled, KD, g, c + 1)
                    nc.vector.tensor_tensor_scan(state[:, c, :], decay[:, c, :], state[:, c, :],
                                                 0.0 if first else carry[:, c:c + 1],
                                                 ALU.mult, ALU.add).then_inc(scanned, 1)
                wait(dve, scanned, KD, g, KD)
                nc.vector.tensor_copy(carry[:, :], state[:, :, GT - 1]).then_inc(carried, 1)

            def finish(g, rows, tiles=range(TILES)):
                for t in tiles:
                    wait(dve, ffn3, TILES, g, t + 1)
                    nc.vector.scalar_tensor_tensor(rows[:, t, :], bank[(Y3 + t) % BANKS][:, :],
                                                   ffn_scale[:, :], rows[:, t, :],
                                                   ALU.mult, ALU.add).then_inc(added3, 1)

            def input_stats(g, parity):
                if isinstance(g, int):
                    dve.wait_ge(loaded_x[parity], 16 * (g // 2 + 1))
                else:
                    dve.wait_ge(loaded_x[parity], 8 * (g - parity) + 16)
                for t in range(TILES):
                    row_stats(0, g, t, x_rows[parity])
                row_moments(0, g)

            def transpose_squares(g, ready, rows, into, made, last_sem, last_g):
                for t in range(TILES):
                    wait(dve, ready, TILES, g, t + 1)
                    if t == 0:
                        wait(dve, last_sem, MOVED, last_g, MOVED)
                    nc.vector.transpose(
                        into[:, :, :, t * SQ:(t + 1) * SQ].rearrange("p r k j -> p k r j").bitcast(u32),
                        rows[:, t, :].rearrange("p (k r j) -> p k r j", r=QUADS, j=SQ).bitcast(u32))\
                      .then_inc(made, 1)

            def squares1(g):
                before = (moved1, g - 1) if isinstance(g, int) and g < 4 else (moved3, g - 4)
                transpose_squares(g, normed[0], norm1, squares, squared_up1, *before)

            def squares3(g, before):
                transpose_squares(g, normed[2], norm3, squares, squared_up3, *before)

            input_stats(0, 0)
            squares1(0)
            dve.wait_ge(loaded_cols, 48)
            nc.vector.tensor_scalar(ba_half[:, :], ba_half[:, :], 0.5, None, ALU.mult)
            nc.vector.tensor_scalar(bx_half[:, :], bx_half[:, :], 0.5, None, ALU.mult)

            def set_scale(peak_count, cols):
                dve.wait_ge(peak_known, peak_count)
                link(nc.vector.tensor_scalar(peak_all[:, cols], peak_all[:, cols], 2.0 ** -96, 2.0 ** 96,
                                             ALU.max, ALU.min))
                link(nc.vector.tensor_scalar(w_inv[:, cols].bitcast(i32), peak_all[:, cols].bitcast(i32),
                                             EXPONENT, None, ALU.bitwise_and))
                link(nc.vector.tensor_scalar(w_scale[:, cols].bitcast(i32), w_inv[:, cols].bitcast(i32),
                                             EXPONENT, None, ALU.bitwise_xor))
                link(nc.vector.tensor_scalar(w_scale[:, cols], w_scale[:, cols], 2.0 ** (TOP - 1), None,
                                             ALU.mult))
                link(nc.vector.tensor_scalar(w_inv[:, cols], w_inv[:, cols], 2.0 ** -TOP, None, ALU.mult))
                nc.vector.tensor_scalar(act_scale[:, cols], w_inv[:, cols], 0.5 / XN, None, ALU.mult)\
                  .then_inc(scale_known, 1)

            def weights_lo(ready, parts):
                dve.wait_ge(w_hi, ready)
                for lo, w, hi, j in parts:
                    last = nc.vector.scalar_tensor_tensor(lo, w, w_scale[:, j:j + 1], hi,
                                                          ALU.mult, ALU.subtract)
                last.then_inc(w_lo, 1)

            def flat(t, j):
                return t[:, 2 * j:2 * j + 2, :].rearrange("p k n -> p (k n)")

            dve.wait_ge(setup_pe, PE_W1)
            for j in range(2):
                link(nc.vector.reduce_max(peak_1[:, j:j + 1], bank[6 + j][:, :], AX.X,
                                          apply_absolute_value=True))
            nc.vector.tensor_tensor(peak[:, W_1:W_1 + 1], peak_1[:, 0:1], peak_1[:, 1:2], ALU.max)\
              .then_inc(peaked, 1)
            set_scale(W1_PEAK, W1_COL)
            weights_lo(W1_READY, [(flat(w1l, j), bank[6 + j][:, :], flat(w1h, j), W_1) for j in range(2)])
            dve.wait_ge(loaded_gates, 32)
            nc.vector.reduce_max(peak[:, W_A:W_A + 1], wa_s[:, :, :], AX.XY, apply_absolute_value=True)
            nc.vector.reduce_max(peak[:, W_X:W_X + 1], wx_s[:, :, :], AX.XY, apply_absolute_value=True)\
              .then_inc(peaked, 1)

            def combine_w2():
                dve.wait_ge(setup_pe, PE_W2)
                dve.wait_ge(loaded_bias, 16)
                link(nc.vector.tensor_tensor(w2_s[:, 0, :], bank[4][:, :], bias_s, ALU.add))
                link(nc.vector.tensor_scalar(w2_s[:, 0, :], w2_s[:, 0, :], sign[:, :], 2.0,
                                             ALU.mult, ALU.mult))
                link(nc.vector.tensor_scalar(w2_s[:, 1, :], bank[5][:, :], sign[:, :], None, ALU.mult))
                nc.vector.reduce_max(peak[:, W_2:W_2 + 1], w2_s, AX.XY, apply_absolute_value=True)\
                  .then_inc(peaked, 1)
                set_scale(W2_PEAK, W2_COL)
                link(nc.vector.tensor_scalar(ffn_scale[:, :], w_inv[:, W2_COL],
                                             0.5 / (2.0 * HIDDEN_SCALE), None, ALU.mult))
                set_scale(GATES_PEAK, GATE_COLS)

            def decay_bias():
                dve.wait_ge(lam_done, 3)
                link(nc.vector.scalar_tensor_tensor(log_a[:, :], lam_col[:, :], 0.0, lam_ln[:, :],
                                                    ALU.min, ALU.subtract))
                link(nc.vector.tensor_scalar(log_a[:, :], log_a[:, :], -0.5 * LOG_C, None, ALU.add))

            def leaves3_lo(g):
                wait(dve, ffn3, TILES, g, 0)
                for k in range(KL):
                    split_lo(leaf3_hi, KL, LEAF3_T, g, k, leaf3h[:, k, :], leaf3l[:, k, :], leaf3_lo)

            def step(s, m, b, c, d, n):
                ga, gb, gc, gd = s, s - 1, s - 2, s - 3
                rows_a, rows_c, rows_d = (res[(m - lag) % UNROLL] for lag in (0, 2, 3))
                head = isinstance(s, int) and s == 0
                second = isinstance(s, int) and s == 1
                if head:
                    input_stats(1, 1)
                    combine_w2()
                    squares1(1)
                tree(ga, gate1, prob1, leaf1, tanh1, tree1, leaf1_t)
                if head:
                    weights_lo(W2_READY, [(w2l[:, :, :], w2_s, w2h[:, :, :], W_2)])
                if n and not head and not second:
                    squares1(s + 1)
                wait(dve, ffn1, TILES, ga, 0)
                for k in range(KL):
                    split_lo(leaf1_hi, KL, LEAF1_T, ga, k, leaf1h[:, k, :], leaf1l[:, k, :], leaf1_lo)
                if second:
                    input_stats(2, 0)
                    squares1(2)
                if c:
                    add_and_stats(2, gc, Y_T, y_t, added2, rows_c, rows_c, None)
                if d:
                    tree(gd, gate3, prob3, leaf3, tanh3, tree3, leaf3_t)
                wait(dve, stored[m], 32 // UNROLL, s - m, 0)
                add_and_stats(1, ga, Y1, ffn1, added1, x_rows[m % 2], rows_a, ffn_scale[:, :])
                if c:
                    squares3(gc, (moved1, ga + 1) if n else (moved3, gc - 1))
                if b:
                    gate_input(gb, 0)
                    gate_input(gb, 1)
                if not head and (not isinstance(s, int) or s + 2 < GROUPS):
                    input_stats(s + 2, m % 2)
                if d:
                    leaves3_lo(gd)
                if b:
                    gate_input(gb, 2)
                if head:
                    weights_lo(GATES_READY, [(wal[:, :, :], wa_s[:, :, :], wah[:, :, :], W_A),
                                             (wxl[:, :, :], wx_s[:, :, :], wxh[:, :, :], W_X)])
                    decay_bias()
                transpose_squares(ga, normed[1], norm2, squares_b, squared_up2, moved2, ga - 1)
                if b:
                    gate_input(gb, 3)
                if d:
                    finish(gd, rows_d, (0, 1))
                if b:
                    for k in range(KD):
                        scale_input(gb, k)
                    scan(gb, (m - 1) % PER_SEQ == 0)
                if d:
                    finish(gd, rows_d, (2, 3))

            steps(dve, step)
            rows_d, rows_p, rows_l = (res[g % UNROLL] for g in (D_LAST, P_LAST, LAST_G))
            add_and_stats(2, P_LAST, Y_T, y_t, added2, rows_p, rows_p, None)
            tree(D_LAST, gate3, prob3, leaf3, tanh3, tree3, leaf3_t)
            squares3(P_LAST, (moved3, D_LAST))
            for c in range(KD - 1):
                gate_input(LAST_G, c)
            leaves3_lo(D_LAST)
            gate_input(LAST_G, KD - 1)
            for c in range(KD):
                scale_input(LAST_G, c)
            scan(LAST_G, LAST_G % PER_SEQ == 0)
            finish(D_LAST, rows_d)
            add_and_stats(2, LAST_G, Y_T, y_t, added2, rows_l, rows_l, None)
            tree(P_LAST, gate3, prob3, leaf3, tanh3, tree3, leaf3_t)
            wait(dve, logits3, 2, LAST_G, 0)
            for k in range(KD):
                wait(dve, n3_hi, KD, LAST_G, k + 1)
                nc.vector.tensor_tensor(n3l[:, k, :], bank[(N3_T + k) % BANKS][:, :], n3h[:, k, :],
                                        ALU.subtract).then_inc(n3_lo, 1)
            leaves3_lo(P_LAST)
            tree(LAST_G, gate3, prob3, leaf3, tanh3, tree3, leaf3_t)
            finish(P_LAST, rows_p)
            leaves3_lo(LAST_G)
            finish(LAST_G, rows_l)

        @block.tensor
        def _(pe):
            pe.wait_ge(sign_made, 1)
            nc.tensor.matmul(bank[7][:, 0:1], sign_row[:, :], one[:, :], start=True, stop=True)\
              .then_inc(setup_pe, 1)
            pe.wait_ge(constants, 3)
            pe.wait_ge(loaded_routers, 32)
            for k in range(KD):
                ch = slice(k * P, k * P + P)
                nc.tensor.transpose(bank[k][:, 0:P], routers_s[:, 0, ch], ident[:, :])
                last = nc.tensor.transpose(bank[k][:, P:NODES], routers_s[0:NODES - P, 1, ch],
                                           ident[0:NODES - P, 0:NODES - P])
            last.then_inc(setup_pe, 1)
            pe.wait_ge(routers_moved, 1 + KD)
            pe.wait_ge(loaded_wq, 16)
            pe.wait_ge(sign_read, 1)
            for j in range(KD):
                for k in range(KD):
                    last = nc.tensor.matmul(bank[6 + j // 2][:, j % 2 * LEAVES:(j % 2 + 1) * LEAVES],
                                            wq_s[:, k, j * P:j * P + P], routers_t[:, k, :],
                                            start=(k == 0), stop=(k == KD - 1))
            last.then_inc(setup_pe, 1)
            pe.wait_ge(differences, 1)
            for k in range(KD):
                ch, at_ = slice(k * P, k * P + P), k % 2 * LEAVES
                nc.tensor.transpose(bank[4 + k // 2][:, at_:at_ + P], even_s[:, ch], ident[:, :])
                last = nc.tensor.transpose(bank[4 + k // 2][:, at_ + P:at_ + LEAVES], odd_s[:, ch], ident[:, :])
            last.then_inc(setup_pe, 1)
            pe.wait_ge(loaded_wout, 16)
            for k in range(KD):
                if k == 2:
                    pe.wait_ge(leaves_moved, 2)
                for j in range(KD):
                    last = nc.tensor.transpose(bank[2 + k][:, j * P:j * P + P],
                                               wout_s[:, j, k * P:k * P + P], ident[:, :])
                if k % 2:
                    last.then_inc(setup_pe, 1)
            pe.wait_ge(wout_moved, KD)
            for j in range(KL):
                for k in range(KD):
                    last = nc.tensor.matmul(bank[4 + j][:, :], leaves_t[:, k, j * P:j * P + P],
                                            wout_t[:, k, :], start=(k == 0), stop=(k == KD - 1))
            last.then_inc(setup_pe, 1)

            def products(out_, early, late, lo_ready, hi_ready=None):
                n = len(early) + len(late)
                last = None
                for q, (l, r) in enumerate(early + late):
                    if q >= len(early):
                        lo_ready(q - len(early))
                    elif hi_ready and q % 2 == 0:
                        hi_ready(q // 2)
                    last = nc.tensor.matmul(out_, l, r, start=(q == 0), stop=(q == n - 1))
                return last

            def by_chunk(semaphore, chunks, g, first=True):
                def ready(k):
                    if first or k == 0:
                        wait(pe, semaphore, chunks, g, k + 1 if first else chunks)
                return ready

            def transposes_to_channels(g, base, rows, ready, done_sem, free):
                for k in range(KD):
                    free(k)
                    if k == 0:
                        wait(pe, ready, TILES, g, TILES)
                    for t in range(TILES):
                        last = nc.tensor.transpose(bank[(base + k) % BANKS][:, t * P:t * P + P],
                                                   rows[:, t, k * P:k * P + P], ident[:, :])
                    last.then_inc(done_sem, 1)

            def tree_logits(g, j, base, nh, nl, hi, lo, done_sem, free):
                free(j)
                for h in range(2):
                    tok = slice((2 * j + h) * P, (2 * j + h + 1) * P)
                    last = products(
                        bank[(base + j) % BANKS][:, h * LEAVES:(h + 1) * LEAVES],
                        [(nh[:, k, tok], w[:, k, :]) for k in range(KD) for w in (w1h, w1l)],
                        [(nl[:, k, tok], w1h[:, k, :]) for k in range(KD)],
                        by_chunk(lo, KD, g, j == h == 0), by_chunk(hi, KD, g) if j == h == 0 else None)
                last.then_inc(done_sem, 1)

            def leaf_transposes(g, base, leaf, tree_sem, done_sem, free):
                for k in range(KL):
                    free(k)
                    wait(pe, tree_sem, TREE, g, TREE - 1 + k)
                    for t in range(TILES):
                        last = nc.tensor.transpose(bank[(base + k) % BANKS][:, t * P:t * P + P],
                                                   leaf[:, t, k * P:k * P + P], ident[:, :])
                    last.then_inc(done_sem, 1)

            def ffn_out(g, base, lh, ll, hi, lo, done_sem, free):
                for t in range(TILES):
                    free(t)
                    tok = slice(t * P, t * P + P)
                    products(bank[(base + t) % BANKS][:, :],
                             [(lh[:, k, tok], w[:, k, :]) for k in range(KL) for w in (w2h, w2l)],
                             [(ll[:, k, tok], w2h[:, k, :]) for k in range(KL)],
                             by_chunk(lo, KL, g, t == 0),
                             by_chunk(hi, KL, g) if t == 0 else None).then_inc(done_sem, 1)

            user = {}

            def free(s, job):
                lag, release, per, k = RELEASES[job]
                before = user.get(job % BANKS)
                user[job % BANKS] = (release, per, s - lag, k)
                if isinstance(s, int) and (s < FIRST or s >= GROUPS):
                    if before:
                        wait(pe, before[0], before[1], before[2], before[3] + 1)
                    return
                before = job - BANKS
                while RELEASES[before % JOBS] is None:
                    before -= BANKS
                lag, release, per, k = RELEASES[before % JOBS]
                wait(pe, release, per, s - lag if before >= 0 else s - 1 - lag, k + 1)

            def first_logits(g, s):
                for j in range(2):
                    tree_logits(g, j, LOGITS1, n1h, n1l, n1_hi, n1_lo, logits1,
                                lambda k: free(s, LOGITS1 + k))

            def r_gate(g, c, s):
                gate(g, c, R_JOB, wah, wal, r_out, s)

            def i_gate(g, c, s):
                gate(g, c, I_JOB, wxh, wxl, i_out, s)

            def gates(g, c, s):
                r_gate(g, c, s)
                i_gate(g, c, s)

            def gate(g, c, jobs, wh, wl, done_sem, s):
                free(s, jobs[c])
                ch = slice(c * P, c * P + P)
                first = done_sem is r_out and c == 0
                products(bank[jobs[c] % BANKS][:, :],
                         [(w[:, k, ch], n2h[:, k, :]) for k in range(KD) for w in (wh, wl)],
                         [(wh[:, k, ch], n2l[:, k, :]) for k in range(KD)],
                         by_chunk(n2_lo, KD, g, first), by_chunk(n2_hi, KD, g) if first else None)\
                    .then_inc(done_sem, 1)

            def y_transposes(g, s):
                for t in range(TILES):
                    free(s, Y_T + t)
                    if t == 0:
                        wait(pe, scanned, KD, g, KD)
                    for c in range(KD):
                        last = nc.tensor.transpose(bank[(Y_T + t) % BANKS][:, c * P:c * P + P],
                                                   state[:, c, t * P:t * P + P], ident[:, :])
                    last.then_inc(y_t, 1)

            def logits_3(g, s, halves=(0, 1)):
                for j in halves:
                    tree_logits(g, j, LOGITS3, n3h, n3l, n3_hi, n3_lo, logits3,
                                lambda k: free(s, LOGITS3 + k))

            def leaves_3(g, s):
                leaf_transposes(g, LEAF3_T, leaf3, tree3, leaf3_t, lambda k: free(s, LEAF3_T + k))

            def ffn_3(g, s):
                ffn_out(g, Y3, leaf3h, leaf3l, leaf3_hi, leaf3_lo, ffn3, lambda t: free(s, Y3 + t))

            def step(s, m, b, c, d, n):
                ga, gb, gc, gd = s, s - 1, s - 2, s - 3
                head = isinstance(s, int) and s == 0
                if head:
                    pe.wait_ge(w_lo, W1_READY)
                first_logits(ga, s)
                if c:
                    y_transposes(gc, s)
                if d:
                    logits_3(gd, s, (0,))
                leaf_transposes(ga, LEAF1_T, leaf1, tree1, leaf1_t, lambda k: free(s, LEAF1_T + k))
                if d:
                    logits_3(gd, s, (1,))
                if head:
                    pe.wait_ge(w_lo, W2_READY)
                ffn_out(ga, Y1, leaf1h, leaf1l, leaf1_hi, leaf1_lo, ffn1, lambda t: free(s, Y1 + t))
                if isinstance(s, int) and s == 1:
                    pe.wait_ge(w_lo, GATES_READY)
                if b:
                    for q in range(KD - 1):
                        gates(gb, q, s)
                if d:
                    leaves_3(gd, s)
                if b:
                    gates(gb, KD - 1, s)
                if d:
                    ffn_3(gd, s)

            steps(pe, step)
            s_1, s_2, s_3 = GROUPS, GROUPS + 1, GROUPS + 2
            y_transposes(P_LAST, s_1)
            logits_3(D_LAST, s_1)
            for c in range(KD - 1):
                gates(LAST_G, c, s_1)
            leaves_3(D_LAST, s_1)
            gates(LAST_G, KD - 1, s_1)
            ffn_3(D_LAST, s_1)
            y_transposes(LAST_G, s_2)
            logits_3(P_LAST, s_2)
            transposes_to_channels(LAST_G, N3_T, norm3, normed[2], n3_t, lambda k: free(s_2, N3_T + k))
            leaves_3(P_LAST, s_2)
            logits_3(LAST_G, s_3)
            ffn_3(P_LAST, s_2)
            leaves_3(LAST_G, s_3)
            ffn_3(LAST_G, s_3)


_INS = ['L0_attn_x', 'L0_attn_Wa', 'L0_attn_Wx', 'L0_attn_ba', 'L0_attn_bx', 'L0_attn_Lam',
        'L0_ffn_Wq', 'L0_ffn_routers', 'L0_ffn_leaf_values', 'L0_ffn_Wout_w', 'L0_ffn_Wout_b']


def kernel(**inputs):
    import concourse.bacc as bacc
    from concourse.bass_utils import run_bass_kernel_spmd

    nc = bacc.Bacc("TRN2", target_bir_lowering=False, num_devices=1)
    arrays, args = {}, []
    for name in _INS:
        a = np.ascontiguousarray(inputs[name])
        arrays[f"in_{name}"] = a
        args.append(nc.dram_tensor(f"in_{name}", a.shape, mybir.dt.from_np(a.dtype), kind="ExternalInput").ap())
    x = arrays["in_L0_attn_x"]
    args.append(nc.dram_tensor("out_x", x.shape, mybir.dt.from_np(x.dtype), kind="ExternalOutput").ap())
    macaron_kernel(nc, *args)
    r = run_bass_kernel_spmd(nc, [arrays], core_ids=[0])
    return r.results[0]["out_x"]
```
